# Optimizing a Trainium2 kernel written in Bass

```python
import numpy as np
import jax
import jax.numpy as jnp

def _softmax(x, axis=-1):
    return jax.nn.softmax(x, axis=axis)

def _gelu(x):
    return jax.nn.gelu(x, approximate=True)

def _silu(x):
    return jax.nn.silu(x)

def _sigmoid(x):
    return jax.nn.sigmoid(x)

def _layernorm(x, axis=-1, eps=1e-05):
    m = jnp.mean(x, axis=axis, keepdims=True)
    v = jnp.var(x, axis=axis, keepdims=True)
    return (x - m) / jnp.sqrt(v + eps)

def _scatter_add(tgt, idx, src, axis=0):
    return tgt.at[idx].add(src)

def _segment_sum(src, seg, n):
    return jax.ops.segment_sum(src, seg, n)
kernel_name = 'mk_gps_d2_gnn_r8_5fede9'

def setup_inputs(seed: int=0):
    np.random.seed(seed)
    _w = jnp.asarray

    def _rec_inputs():
        import jax
        import jax.numpy as jnp
        _gk = jax.random.key(seed)
        x = -0.0003713 + 1 * jax.random.normal(jax.random.fold_in(_gk, 1), (6250, 256), jnp.float32)
        src = jax.random.randint(jax.random.fold_in(_gk, 2), (100000,), 0, 6250, jnp.int32)
        dst = jax.random.randint(jax.random.fold_in(_gk, 3), (100000,), 0, 6250, jnp.int32)
        _o = jnp.argsort(dst, stable=True)
        src = src[_o]
        dst = dst[_o]
        edge_attr_16 = 0.000254156 + 0.999948 * jax.random.normal(jax.random.fold_in(_gk, 12), (100000, 16), jnp.float32)
        edge_type_16 = jax.random.randint(jax.random.fold_in(_gk, 14), (100000,), 0, 16, jnp.int32)
        return (x, src, dst, edge_attr_16, edge_type_16)
    x, src, dst, edge_attr_16, edge_type_16 = _rec_inputs()

    def _L0_gnn_setup():
        import jax, jax.numpy as jnp
        import numpy as np
        N, D, H = (6250, 256, 8)
        HD = D // H
        E = 100000
        NEG_SLOPE = 0.2

        def _gat_layer(x, edge_index, W, att_src, att_dst, bias, ln_g, ln_b, W1, b1, W2, b2):
            n = x.shape[0]
            sl = jnp.arange(n, dtype=edge_index.dtype)
            src = jnp.concatenate([edge_index[0], sl])
            dst = jnp.concatenate([edge_index[1], sl])
            xp = (x @ W).reshape(n, H, HD)
            a_src = jnp.einsum('nhd,hd->nh', xp, att_src)
            a_dst = jnp.einsum('nhd,hd->nh', xp, att_dst)
            e = a_src[src] + a_dst[dst]
            e = jax.nn.leaky_relu(e, NEG_SLOPE)
            m = jax.ops.segment_max(e, dst, num_segments=n)
            ex = jnp.exp(e - m[dst])
            denom = jax.ops.segment_sum(ex, dst, num_segments=n)
            alpha = ex / (denom[dst] + 1e-16)
            msg = alpha[:, :, None] * xp[src]
            out = jax.ops.segment_sum(msg, dst, num_segments=n)
            h = out.reshape(n, D) + bias
            r = h + x
            mu = jnp.mean(r, axis=-1, keepdims=True)
            var = jnp.mean(jnp.square(r - mu), axis=-1, keepdims=True)
            hn = (r - mu) / jnp.sqrt(var + 1e-05) * ln_g + ln_b
            return jax.nn.relu(hn @ W1 + b1) @ W2 + b2
        key = jax.random.key(seed)
        ks = jax.random.split(key, 12)
        s = 1.0 / np.sqrt(D)
        return {'x': jax.random.normal(ks[0], (N, D), jnp.float32), 'edge_index': jax.random.randint(ks[1], (2, E), 0, N, jnp.int64), 'edge_attr': jax.random.normal(ks[2], (E, 16), jnp.float32), 'W': jax.random.normal(ks[3], (D, D), jnp.float32) * s, 'att_src': jax.random.normal(ks[4], (H, HD), jnp.float32) * s, 'att_dst': jax.random.normal(ks[5], (H, HD), jnp.float32) * s, 'bias': jnp.zeros((D,), jnp.float32), 'ln_g': jnp.ones((D,), jnp.float32), 'ln_b': jnp.zeros((D,), jnp.float32), 'W1': jax.random.normal(ks[6], (D, D), jnp.float32) * s, 'b1': jnp.zeros((D,), jnp.float32), 'W2': jax.random.normal(ks[7], (D, D), jnp.float32) * s, 'b2': jnp.zeros((D,), jnp.float32)}
    _L0_gnn_all = _L0_gnn_setup()
    _L0_gnn_in = {k: v for k, v in _L0_gnn_all.items() if k in ('W', 'att_src', 'att_dst', 'bias', 'ln_g', 'ln_b', 'W1', 'b1', 'W2', 'b2')}
    del _L0_gnn_all

    def _L0_mix_setup():
        import math
        import jax, jax.numpy as jnp
        import numpy as np
        EPS_DIV = 1e-07
        EPS_NORM = 1e-12

        def _l2_normalize(x, axis):
            n = jnp.sqrt(jnp.sum(x * x, axis=axis, keepdims=True))
            return x / jnp.maximum(n, EPS_NORM)
        key = jax.random.key(seed)
        ks = jax.random.split(key, 5)
        b, N, C = (8, 512, 256)
        x = jax.random.normal(ks[0], (b, N, C), dtype=jnp.float32)
        W_qkv = jax.random.normal(ks[1], (C, 3 * C), dtype=jnp.float32) * (1.0 / math.sqrt(C))
        b_qkv = jax.random.normal(ks[2], (3 * C,), dtype=jnp.float32) * 0.02
        W_out = jax.random.normal(ks[3], (C, C), dtype=jnp.float32) * (1.0 / math.sqrt(C))
        b_out = jax.random.normal(ks[4], (C,), dtype=jnp.float32) * 0.02
        return {'x': x, 'W_qkv': W_qkv, 'b_qkv': b_qkv, 'W_out': W_out, 'b_out': b_out}
    _L0_mix_all = _L0_mix_setup()
    _L0_mix_in = {k: v for k, v in _L0_mix_all.items() if k in ('W_qkv', 'b_qkv', 'W_out', 'b_out')}
    del _L0_mix_all

    def _L0_ffn_setup():
        import jax, jax.numpy as jnp
        import numpy as np
        DIM = 256
        H = 8
        D = 64
        G = 64
        INNER = H * D
        SCALE = D ** (-0.5)
        key = jax.random.key(seed)
        ks = jax.random.split(key, 12)
        B, N = (4, 2048)
        x = jax.random.normal(ks[0], (B, N, DIM), dtype=jnp.float32)
        s = lambda fan_in: 1.0 / np.sqrt(fan_in)
        W_fx = jax.random.normal(ks[1], (DIM, INNER), dtype=jnp.float32) * s(DIM)
        b_fx = jnp.zeros((INNER,), dtype=jnp.float32)
        W_x = jax.random.normal(ks[2], (DIM, INNER), dtype=jnp.float32) * s(DIM)
        b_x = jnp.zeros((INNER,), dtype=jnp.float32)
        A = jax.random.normal(ks[3], (G, D), dtype=jnp.float32)
        Q, _ = jnp.linalg.qr(A.T)
        W_slice = Q[:, :G].astype(jnp.float32)
        b_slice = jnp.zeros((G,), dtype=jnp.float32)
        W_q = jax.random.normal(ks[4], (D, D), dtype=jnp.float32) * s(D)
        W_k = jax.random.normal(ks[5], (D, D), dtype=jnp.float32) * s(D)
        W_v = jax.random.normal(ks[6], (D, D), dtype=jnp.float32) * s(D)
        W_out = jax.random.normal(ks[7], (INNER, DIM), dtype=jnp.float32) * s(INNER)
        b_out = jnp.zeros((DIM,), dtype=jnp.float32)
        temperature = jnp.ones((1, H, 1, 1), dtype=jnp.float32) * 0.5
        return {'x': x, 'W_fx': W_fx, 'b_fx': b_fx, 'W_x': W_x, 'b_x': b_x, 'W_slice': W_slice, 'b_slice': b_slice, 'W_q': W_q, 'W_k': W_k, 'W_v': W_v, 'W_out': W_out, 'b_out': b_out, 'temperature': temperature}
    _L0_ffn_all = _L0_ffn_setup()
    _L0_ffn_in = {k: v for k, v in _L0_ffn_all.items() if k in ('W_fx', 'b_fx', 'W_x', 'b_x', 'W_slice', 'b_slice', 'W_q', 'W_k', 'W_v', 'W_out', 'b_out', 'temperature')}
    del _L0_ffn_all

    def _L1_gnn_setup():
        import jax, jax.numpy as jnp
        import numpy as np
        N_NODES = 6250
        N_EDGES = 100000
        HDIM = 256
        NUMRELS = 16

        def _gru_cell(x, h, w_ih, w_hh, b_ih, b_hh):
            gi = x @ w_ih.T + b_ih
            gh = h @ w_hh.T + b_hh
            i_r, i_z, i_n = jnp.split(gi, 3, axis=-1)
            h_r, h_z, h_n = jnp.split(gh, 3, axis=-1)
            r = jax.nn.sigmoid(i_r + h_r)
            z = jax.nn.sigmoid(i_z + h_z)
            n = jnp.tanh(i_n + r * h_n)
            return (1.0 - z) * n + z * h
        key = jax.random.key(seed)
        ks = jax.random.split(key, 9)
        h = jax.random.normal(ks[0], (N_NODES, HDIM), dtype=jnp.float32)
        relvectors = jax.random.normal(ks[1], (NUMRELS, HDIM), dtype=jnp.float32)
        s = 1.0 / np.sqrt(HDIM)
        w_ih = jax.random.uniform(ks[2], (3 * HDIM, HDIM), minval=-s, maxval=s, dtype=jnp.float32)
        w_hh = jax.random.uniform(ks[3], (3 * HDIM, HDIM), minval=-s, maxval=s, dtype=jnp.float32)
        b_ih = jax.random.uniform(ks[4], (3 * HDIM,), minval=-s, maxval=s, dtype=jnp.float32)
        b_hh = jax.random.uniform(ks[5], (3 * HDIM,), minval=-s, maxval=s, dtype=jnp.float32)
        edge_src = jax.random.randint(ks[6], (N_EDGES,), 0, N_NODES, dtype=jnp.int32)
        edge_dst = jax.random.randint(ks[7], (N_EDGES,), 0, N_NODES, dtype=jnp.int32)
        edge_rel = jax.random.randint(ks[8], (N_EDGES,), 0, NUMRELS, dtype=jnp.int32)
        return {'h': h, 'relvectors': relvectors, 'w_ih': w_ih, 'w_hh': w_hh, 'b_ih': b_ih, 'b_hh': b_hh, 'edge_src': edge_src, 'edge_dst': edge_dst, 'edge_rel': edge_rel}
    _L1_gnn_all = _L1_gnn_setup()
    _L1_gnn_in = {k: v for k, v in _L1_gnn_all.items() if k in ('relvectors', 'w_ih', 'w_hh', 'b_ih', 'b_hh')}
    del _L1_gnn_all

    def _L1_mix_setup():
        import jax, jax.numpy as jnp
        import numpy as np
        MIDC = 256
        HEADS = 8
        HEADC = MIDC // HEADS
        EPS = 1e-05

        def _ln(x, gamma, beta):
            mu = jnp.mean(x, axis=-1, keepdims=True)
            var = jnp.var(x, axis=-1, keepdims=True)
            return (x - mu) * jax.lax.rsqrt(var + EPS) * gamma + beta
        key = jax.random.key(seed)
        ks = jax.random.split(key, 8)
        B, HW, C = (8, 512, MIDC)
        s = 1.0 / np.sqrt(C)
        return {'x': jax.random.normal(ks[0], (B, HW, C), jnp.float32), 'w_qkv': jax.random.normal(ks[1], (C, 3 * C), jnp.float32) * s, 'b_qkv': jnp.zeros((3 * C,), jnp.float32), 'kln_g': jnp.ones((HEADC,), jnp.float32), 'kln_b': jnp.zeros((HEADC,), jnp.float32), 'vln_g': jnp.ones((HEADC,), jnp.float32), 'vln_b': jnp.zeros((HEADC,), jnp.float32), 'w1': jax.random.normal(ks[2], (C, C), jnp.float32) * s, 'b1': jnp.zeros((C,), jnp.float32), 'w2': jax.random.normal(ks[3], (C, C), jnp.float32) * s, 'b2': jnp.zeros((C,), jnp.float32)}
    _L1_mix_all = _L1_mix_setup()
    _L1_mix_in = {k: v for k, v in _L1_mix_all.items() if k in ('w_qkv', 'b_qkv', 'kln_g', 'kln_b', 'vln_g', 'vln_b', 'w1', 'b1', 'w2', 'b2')}
    del _L1_mix_all

    def _L1_ffn_setup():
        import jax, jax.numpy as jnp
        import numpy as np
        NUM_EXPERTS = 8
        TOP_K = 2
        B, S, D = (8, 1024, 256)

        def _moe(tokens, router_w, w1, b1, w2, b2):
            N = tokens.shape[0]
            E = router_w.shape[0]
            logits = tokens.astype(jnp.float32) @ router_w.astype(jnp.float32).T
            probs = jax.nn.softmax(logits, axis=-1)
            rw, re = jax.lax.top_k(probs, TOP_K)
            if TOP_K > 1:
                rw = rw / jnp.maximum(rw.sum(-1, keepdims=True), 1e-12)
            rw = rw.astype(tokens.dtype)
            combine = jnp.zeros((N, E), tokens.dtype).at[jnp.arange(N)[:, None], re].set(rw)
            out = tokens
            for e in range(E):
                h = jax.nn.gelu(tokens @ w1[e] + b1[e], approximate=False)
                y = h @ w2[e] + b2[e]
                out = out + combine[:, e:e + 1] * y
            return out
        key = jax.random.key(seed)
        ks = jax.random.split(key, 4)
        scale = 1.0 / np.sqrt(D).astype(np.float32)
        return {'input_embeddings': jax.random.normal(ks[0], (B, S, D), jnp.float32), 'router_w': jax.random.normal(ks[1], (NUM_EXPERTS, D), jnp.float32) * scale, 'w1': jax.random.normal(ks[2], (NUM_EXPERTS, D, D), jnp.float32) * scale, 'b1': jnp.zeros((NUM_EXPERTS, D), jnp.float32), 'w2': jax.random.normal(ks[3], (NUM_EXPERTS, D, D), jnp.float32) * scale, 'b2': jnp.zeros((NUM_EXPERTS, D), jnp.float32)}
    _L1_ffn_all = _L1_ffn_setup()
    _L1_ffn_in = {k: v for k, v in _L1_ffn_all.items() if k in ('router_w', 'w1', 'b1', 'w2', 'b2')}
    del _L1_ffn_all
    return {'x': x, 'src': src, 'dst': dst, 'edge_attr_16': edge_attr_16, 'edge_type_16': edge_type_16, 'L0_gnn_W': _L0_gnn_in['W'], 'L0_gnn_att_src': _L0_gnn_in['att_src'], 'L0_gnn_att_dst': _L0_gnn_in['att_dst'], 'L0_gnn_bias': _L0_gnn_in['bias'], 'L0_gnn_ln_g': _L0_gnn_in['ln_g'], 'L0_gnn_ln_b': _L0_gnn_in['ln_b'], 'L0_gnn_W1': _L0_gnn_in['W1'], 'L0_gnn_b1': _L0_gnn_in['b1'], 'L0_gnn_W2': _L0_gnn_in['W2'], 'L0_gnn_b2': _L0_gnn_in['b2'], 'L0_mix_W_qkv': _L0_mix_in['W_qkv'], 'L0_mix_b_qkv': _L0_mix_in['b_qkv'], 'L0_mix_W_out': _L0_mix_in['W_out'], 'L0_mix_b_out': _L0_mix_in['b_out'], 'L0_ffn_W_fx': _L0_ffn_in['W_fx'], 'L0_ffn_b_fx': _L0_ffn_in['b_fx'], 'L0_ffn_W_x': _L0_ffn_in['W_x'], 'L0_ffn_b_x': _L0_ffn_in['b_x'], 'L0_ffn_W_slice': _L0_ffn_in['W_slice'], 'L0_ffn_b_slice': _L0_ffn_in['b_slice'], 'L0_ffn_W_q': _L0_ffn_in['W_q'], 'L0_ffn_W_k': _L0_ffn_in['W_k'], 'L0_ffn_W_v': _L0_ffn_in['W_v'], 'L0_ffn_W_out': _L0_ffn_in['W_out'], 'L0_ffn_b_out': _L0_ffn_in['b_out'], 'L0_ffn_temperature': _L0_ffn_in['temperature'], 'L1_gnn_relvectors': _L1_gnn_in['relvectors'], 'L1_gnn_w_ih': _L1_gnn_in['w_ih'], 'L1_gnn_w_hh': _L1_gnn_in['w_hh'], 'L1_gnn_b_ih': _L1_gnn_in['b_ih'], 'L1_gnn_b_hh': _L1_gnn_in['b_hh'], 'L1_mix_w_qkv': _L1_mix_in['w_qkv'], 'L1_mix_b_qkv': _L1_mix_in['b_qkv'], 'L1_mix_kln_g': _L1_mix_in['kln_g'], 'L1_mix_kln_b': _L1_mix_in['kln_b'], 'L1_mix_vln_g': _L1_mix_in['vln_g'], 'L1_mix_vln_b': _L1_mix_in['vln_b'], 'L1_mix_w1': _L1_mix_in['w1'], 'L1_mix_b1': _L1_mix_in['b1'], 'L1_mix_w2': _L1_mix_in['w2'], 'L1_mix_b2': _L1_mix_in['b2'], 'L1_ffn_router_w': _L1_ffn_in['router_w'], 'L1_ffn_w1': _L1_ffn_in['w1'], 'L1_ffn_b1': _L1_ffn_in['b1'], 'L1_ffn_w2': _L1_ffn_in['w2'], 'L1_ffn_b2': _L1_ffn_in['b2']}

def reference(x, src, dst, edge_attr_16, edge_type_16, L0_gnn_W, L0_gnn_att_src, L0_gnn_att_dst, L0_gnn_bias, L0_gnn_ln_g, L0_gnn_ln_b, L0_gnn_W1, L0_gnn_b1, L0_gnn_W2, L0_gnn_b2, L0_mix_W_qkv, L0_mix_b_qkv, L0_mix_W_out, L0_mix_b_out, L0_ffn_W_fx, L0_ffn_b_fx, L0_ffn_W_x, L0_ffn_b_x, L0_ffn_W_slice, L0_ffn_b_slice, L0_ffn_W_q, L0_ffn_W_k, L0_ffn_W_v, L0_ffn_W_out, L0_ffn_b_out, L0_ffn_temperature, L1_gnn_relvectors, L1_gnn_w_ih, L1_gnn_w_hh, L1_gnn_b_ih, L1_gnn_b_hh, L1_mix_w_qkv, L1_mix_b_qkv, L1_mix_kln_g, L1_mix_kln_b, L1_mix_vln_g, L1_mix_vln_b, L1_mix_w1, L1_mix_b1, L1_mix_w2, L1_mix_b2, L1_ffn_router_w, L1_ffn_w1, L1_ffn_b1, L1_ffn_w2, L1_ffn_b2):
    import jax
    import jax.numpy as jnp

    def _L0_gnn_ref(x, edge_index, edge_attr, W, att_src, att_dst, bias, ln_g, ln_b, W1, b1, W2, b2):
        import jax, jax.numpy as jnp
        import numpy as np
        N, D, H = (6250, 256, 8)
        HD = D // H
        E = 100000
        NEG_SLOPE = 0.2

        def _gat_layer(x, edge_index, W, att_src, att_dst, bias, ln_g, ln_b, W1, b1, W2, b2):
            n = x.shape[0]
            sl = jnp.arange(n, dtype=edge_index.dtype)
            src = jnp.concatenate([edge_index[0], sl])
            dst = jnp.concatenate([edge_index[1], sl])
            xp = (x @ W).reshape(n, H, HD)
            a_src = jnp.einsum('nhd,hd->nh', xp, att_src)
            a_dst = jnp.einsum('nhd,hd->nh', xp, att_dst)
            e = a_src[src] + a_dst[dst]
            e = jax.nn.leaky_relu(e, NEG_SLOPE)
            m = jax.ops.segment_max(e, dst, num_segments=n)
            ex = jnp.exp(e - m[dst])
            denom = jax.ops.segment_sum(ex, dst, num_segments=n)
            alpha = ex / (denom[dst] + 1e-16)
            msg = alpha[:, :, None] * xp[src]
            out = jax.ops.segment_sum(msg, dst, num_segments=n)
            h = out.reshape(n, D) + bias
            r = h + x
            mu = jnp.mean(r, axis=-1, keepdims=True)
            var = jnp.mean(jnp.square(r - mu), axis=-1, keepdims=True)
            hn = (r - mu) / jnp.sqrt(var + 1e-05) * ln_g + ln_b
            return jax.nn.relu(hn @ W1 + b1) @ W2 + b2
        return _gat_layer(x, edge_index, W, att_src, att_dst, bias, ln_g, ln_b, W1, b1, W2, b2)

    def _L0_mix_ref(x, W_qkv, b_qkv, W_out, b_out):
        import math
        import jax, jax.numpy as jnp
        import numpy as np
        EPS_DIV = 1e-07
        EPS_NORM = 1e-12

        def _l2_normalize(x, axis):
            n = jnp.sqrt(jnp.sum(x * x, axis=axis, keepdims=True))
            return x / jnp.maximum(n, EPS_NORM)
        b, N, C = x.shape
        qkv = x @ W_qkv + b_qkv
        q, k, v = jnp.split(qkv, 3, axis=2)
        q = q - jnp.mean(q, axis=2, keepdims=True)
        k = k - jnp.mean(k, axis=2, keepdims=True)
        q2 = q * q
        k2 = k * k
        q2s = jnp.sum(q2, axis=2, keepdims=True)
        k2s = jnp.sum(k2, axis=2, keepdims=True)
        k2 = _l2_normalize(k2 / (k2s + EPS_DIV), axis=-2)
        q2 = _l2_normalize(q2 / (q2s + EPS_DIV), axis=-1)
        kv = jnp.einsum('bnc,bnd->bcd', k2, v)
        t2 = jnp.einsum('bnc,bcd->bnd', q2, kv) / math.sqrt(N)
        attn = v + t2
        return attn @ W_out + b_out

    def _L0_ffn_ref(x, W_fx, b_fx, W_x, b_x, W_slice, b_slice, W_q, W_k, W_v, W_out, b_out, temperature):
        import jax, jax.numpy as jnp
        import numpy as np
        DIM = 256
        H = 8
        D = 64
        G = 64
        INNER = H * D
        SCALE = D ** (-0.5)
        B, N, _ = x.shape
        fx_mid = (x @ W_fx + b_fx).reshape(B, N, H, D).transpose(0, 2, 1, 3)
        x_mid = (x @ W_x + b_x).reshape(B, N, H, D).transpose(0, 2, 1, 3)
        temp = jnp.clip(temperature, 0.1, 5.0)
        slice_weights = jax.nn.softmax((x_mid @ W_slice + b_slice) / temp, axis=-1)
        slice_norm = slice_weights.sum(axis=2)
        slice_token = jnp.einsum('bhnc,bhng->bhgc', fx_mid, slice_weights)
        slice_token = slice_token / (slice_norm[..., None] + 1e-05)
        q = slice_token @ W_q
        k = slice_token @ W_k
        v = slice_token @ W_v
        attn = jax.nn.softmax(jnp.einsum('bhgc,bhkc->bhgk', q, k) * SCALE, axis=-1)
        out_slice = jnp.einsum('bhgk,bhkc->bhgc', attn, v)
        out_x = jnp.einsum('bhgc,bhng->bhnc', out_slice, slice_weights)
        out_x = out_x.transpose(0, 2, 1, 3).reshape(B, N, INNER)
        return out_x @ W_out + b_out

    def _L1_gnn_ref(h, relvectors, w_ih, w_hh, b_ih, b_hh, edge_src, edge_dst, edge_rel):
        import jax, jax.numpy as jnp
        import numpy as np
        N_NODES = 6250
        N_EDGES = 100000
        HDIM = 256
        NUMRELS = 16

        def _gru_cell(x, h, w_ih, w_hh, b_ih, b_hh):
            gi = x @ w_ih.T + b_ih
            gh = h @ w_hh.T + b_hh
            i_r, i_z, i_n = jnp.split(gi, 3, axis=-1)
            h_r, h_z, h_n = jnp.split(gh, 3, axis=-1)
            r = jax.nn.sigmoid(i_r + h_r)
            z = jax.nn.sigmoid(i_z + h_z)
            n = jnp.tanh(i_n + r * h_n)
            return (1.0 - z) * n + z * h
        msg = h[edge_src] + relvectors[edge_rel]
        red = jax.ops.segment_sum(msg, edge_dst, num_segments=h.shape[0])
        return _gru_cell(red, h, w_ih, w_hh, b_ih, b_hh)

    def _L1_mix_ref(x, w_qkv, b_qkv, kln_g, kln_b, vln_g, vln_b, w1, b1, w2, b2):
        import jax, jax.numpy as jnp
        import numpy as np
        MIDC = 256
        HEADS = 8
        HEADC = MIDC // HEADS
        EPS = 1e-05

        def _ln(x, gamma, beta):
            mu = jnp.mean(x, axis=-1, keepdims=True)
            var = jnp.var(x, axis=-1, keepdims=True)
            return (x - mu) * jax.lax.rsqrt(var + EPS) * gamma + beta
        B, HW, C = x.shape
        bias = x
        qkv = (x @ w_qkv + b_qkv).reshape(B, HW, HEADS, 3 * HEADC)
        qkv = qkv.transpose(0, 2, 1, 3)
        q, k, v = jnp.split(qkv, 3, axis=-1)
        k = _ln(k, kln_g, kln_b)
        v = _ln(v, vln_g, vln_b)
        kv = jnp.einsum('bhnd,bhne->bhde', k, v) / HW
        out = jnp.einsum('bhnd,bhde->bhne', q, kv)
        out = out.transpose(0, 2, 1, 3).reshape(B, HW, C)
        ret = out + bias
        h = jax.nn.gelu(ret @ w1 + b1, approximate=False)
        return h @ w2 + b2 + bias

    def _L1_ffn_ref(input_embeddings, router_w, w1, b1, w2, b2):
        import jax, jax.numpy as jnp
        import numpy as np
        NUM_EXPERTS = 8
        TOP_K = 2
        B, S, D = (8, 1024, 256)

        def _moe(tokens, router_w, w1, b1, w2, b2):
            N = tokens.shape[0]
            E = router_w.shape[0]
            logits = tokens.astype(jnp.float32) @ router_w.astype(jnp.float32).T
            probs = jax.nn.softmax(logits, axis=-1)
            rw, re = jax.lax.top_k(probs, TOP_K)
            if TOP_K > 1:
                rw = rw / jnp.maximum(rw.sum(-1, keepdims=True), 1e-12)
            rw = rw.astype(tokens.dtype)
            combine = jnp.zeros((N, E), tokens.dtype).at[jnp.arange(N)[:, None], re].set(rw)
            out = tokens
            for e in range(E):
                h = jax.nn.gelu(tokens @ w1[e] + b1[e], approximate=False)
                y = h @ w2[e] + b2[e]
                out = out + combine[:, e:e + 1] * y
            return out
        b, s, d = input_embeddings.shape
        tokens = input_embeddings.reshape(b * s, d)
        return _moe(tokens, router_w, w1, b1, w2, b2).reshape(b, s, d)
    edge_index = jnp.stack([src, dst])
    xn = _layernorm(x, axis=-1)
    x = x + _L0_gnn_ref(xn, edge_index, edge_attr_16, L0_gnn_W, L0_gnn_att_src, L0_gnn_att_dst, L0_gnn_bias, L0_gnn_ln_g, L0_gnn_ln_b, L0_gnn_W1, L0_gnn_b1, L0_gnn_W2, L0_gnn_b2) + _L0_mix_ref(xn[None], L0_mix_W_qkv, L0_mix_b_qkv, L0_mix_W_out, L0_mix_b_out)[0]
    x = x + _L0_ffn_ref(_layernorm(x, axis=-1)[None], L0_ffn_W_fx, L0_ffn_b_fx, L0_ffn_W_x, L0_ffn_b_x, L0_ffn_W_slice, L0_ffn_b_slice, L0_ffn_W_q, L0_ffn_W_k, L0_ffn_W_v, L0_ffn_W_out, L0_ffn_b_out, L0_ffn_temperature)[0]
    xn = _layernorm(x, axis=-1)
    x = x + _L1_gnn_ref(xn, L1_gnn_relvectors, L1_gnn_w_ih, L1_gnn_w_hh, L1_gnn_b_ih, L1_gnn_b_hh, src, dst, edge_type_16) + _L1_mix_ref(xn[None], L1_mix_w_qkv, L1_mix_b_qkv, L1_mix_kln_g, L1_mix_kln_b, L1_mix_vln_g, L1_mix_vln_b, L1_mix_w1, L1_mix_b1, L1_mix_w2, L1_mix_b2)[0]
    x = x + _L1_ffn_ref(_layernorm(x, axis=-1)[None], L1_ffn_router_w, L1_ffn_w1, L1_ffn_b1, L1_ffn_w2, L1_ffn_b2)[0]
    return x

_drawn_inputs = setup_inputs


def setup_inputs(seed=0):
    import zlib

    import numpy as np

    out = dict(_drawn_inputs(seed))
    spreads = {'L0_gnn_bias': (0.0, 0.1),
     'L0_gnn_ln_g': (1.0, 0.2),
     'L0_gnn_ln_b': (0.0, 0.1),
     'L0_gnn_b1': (0.0, 0.1),
     'L0_gnn_b2': (0.0, 0.1),
     'L0_ffn_b_fx': (0.0, 0.1),
     'L0_ffn_b_x': (0.0, 0.8),
     'L0_ffn_b_slice': (0.0, 0.8),
     'L0_ffn_b_out': (0.0, 0.1),
     'L0_ffn_temperature': (0.5, 0.6),
     'L1_mix_b_qkv': (0.0, 0.1),
     'L1_mix_kln_g': (1.0, 0.2),
     'L1_mix_kln_b': (0.0, 0.1),
     'L1_mix_vln_g': (1.0, 0.2),
     'L1_mix_vln_b': (0.0, 0.1),
     'L1_mix_b1': (0.0, 0.317),
     'L1_mix_b2': (0.0, 0.1),
     'L1_ffn_b1': (0.0, 0.678),
     'L1_ffn_b2': (0.0, 0.469)}
    factors = {'L0_gnn_att_dst': 4.146,
     'L0_ffn_W_x': 4.526,
     'L0_ffn_W_slice': 7.348,
     'L0_ffn_W_q': 8.0,
     'L0_ffn_W_k': 8.0,
     'L1_gnn_b_ih': 8.0,
     'L1_gnn_b_hh': 8.0}
    for name, (base, spread) in spreads.items():
        noise = np.random.default_rng([zlib.crc32(name.encode()), seed]).standard_normal(out[name].shape)
        drawn = base * np.exp(spread * noise) if base else spread * noise
        out[name] = jnp.asarray(drawn.astype(out[name].dtype))
    for name, factor in factors.items():
        out[name] = (out[name] * factor).astype(out[name].dtype)
    return out
```

```python
from contextlib import ExitStack

import numpy as np
import concourse.bass as bass
from concourse import mybir
from concourse.alu_op_type import AluOpType as ALU

F32 = mybir.dt.float32
I32 = mybir.dt.int32
U32 = mybir.dt.uint32
ACT = mybir.ActivationFunctionType
AX = mybir.AxisListType.X
ds = bass.ds

N, D, H, HD = 6250, 256, 8, 32
P = 125
NT = N // P
PAIRS = NT // 2
E = 100000
ET = 4
HT = ET // 2
EG = ET * P
NG = E // EG
NREL = 16
GATW = D + H
RELW = D + NREL
FAR = 1000.0
GUARD = 70.0
EPS = 1e-5
S = 64
NEXP = 8
assert NT * P == N and NG * EG == E and PAIRS * 2 == NT


class Mem:

    def __init__(self, nc, ctx):
        self.nc, self.ctx, self.sems = nc, ctx, []

    def sb(self, name, shape, dt=F32):
        return self.ctx.enter_context(self.nc.sbuf_tensor(name, shape, dt))

    def bank(self, name):
        return self.ctx.enter_context(self.nc.psum_tensor(name, [128, 512], F32))

    def sem(self, name):
        if not self.sems:
            self.ctx.callback(self.clear)
        self.sems.append(self.nc.alloc_semaphore(name))
        return self.sems[-1]

    def clear(self):
        self.nc.clear_and_free_semaphores(self.sems)
        self.nc.all_engine_barrier()


class Steps:

    def __init__(self, eng, sem, base=0):
        self.eng, self.sem, self.base, self.n = eng, sem, base, 0

    def mark(self, ins):
        ins.then_inc(self.sem, 1)
        self.n += 1

    def wait(self):
        self.eng.wait_ge(self.sem, self.base + self.n)

    def link(self, ins):
        self.mark(ins)
        self.wait()


def load_phase(nc, name, copies):
    with ExitStack() as ctx:
        m = Mem(nc, ctx)
        s_sp, s_act = m.sem(f"{name}_landed_sp"), m.sem(f"{name}_landed_act")
        block = ctx.enter_context(nc.Block())
        mine, other = copies[0::2], copies[1::2]

        @block.sync
        def _(sp):
            for dst, src in mine:
                sp.dma_start(dst, src).then_inc(s_sp, 16)
            sp.wait_ge(s_sp, 16 * len(mine))

        @block.scalar
        def _(act):
            for dst, src in other:
                act.dma_start(dst, src).then_inc(s_act, 16)
            if other:
                act.wait_ge(s_act, 16 * len(other))


def rows(w):
    return w.rearrange("(b p) n -> p b n", p=128)


def wide(v, n=128):
    return v.rearrange("(a n) -> a n", a=1).partition_broadcast(n)


def constants_phase(nc, g):
    with ExitStack() as ctx:
        m = Mem(nc, ctx)
        s_made = m.sem("const_made")
        block = ctx.enter_context(nc.Block())

        @block.gpsimd
        def _(pool):
            st = Steps(pool, s_made)
            st.mark(pool.memset(g.ident[:, :], 0.0))
            st.mark(pool.memset(g.ones[:, :], 1.0))
            st.mark(pool.memset(g.zeros[:, :], 0.0))
            st.mark(pool.iota(g.iota_i[:, :], [[1, 256]], 0, 0))
            st.mark(pool.iota(g.chan_i[:, :], [[0, 1]], 0, 1))
            st.mark(pool.iota(g.tile_i[:, :], [[P, NT]], 0, 0))
            st.link(pool.memset(g.before[:, :], 0.0))
            st.mark(pool.affine_select(g.ident[:, :], g.ident[:, :], [[-1, 128]], ALU.not_equal, 1.0, 0, 1))
            st.mark(pool.affine_select(g.before[:, :], g.before[:, :], [[-1, NT]], ALU.is_ge, 1.0, 0, 1))
            st.mark(pool.tensor_copy(g.iota[:, :], g.iota_i[:, :]))
            st.mark(pool.tensor_copy(g.chan[:, :], g.chan_i[:, :]))
            st.link(pool.tensor_copy(g.tile0[:, :], g.tile_i[:, :]))


def scales_phase(nc, name, halves, rstd, shift):
    with ExitStack() as ctx:
        m = Mem(nc, ctx)
        s_dve, s_var, s_root = m.sem(f"{name}_dve"), m.sem(f"{name}_var"), m.sem(f"{name}_root")
        mean, dif, dev = (m.sb(f"{name}_{n}", [128, NT]) for n in ("mean", "dif", "dev"))
        even, odd = halves[:P, :, 1], halves[:P, :, 4]
        block = ctx.enter_context(nc.Block())

        @block.vector
        def _(dve):
            st = Steps(dve, s_dve)
            st.mark(dve.tensor_tensor(mean[:P, :], even, odd, ALU.add))
            st.mark(dve.tensor_tensor(dif[:P, :], even, odd, ALU.subtract))
            st.link(dve.tensor_tensor(dev[:P, :], halves[:P, :, 2], halves[:P, :, 5], ALU.add))
            st.mark(dve.scalar_tensor_tensor(dif[:P, :], dif[:P, :], 0.25, dif[:P, :], ALU.mult, ALU.mult))
            st.link(dve.tensor_scalar(dev[:P, :], dev[:P, :], 1.0 / D, EPS, ALU.mult, ALU.add))
            dve.tensor_tensor(dev[:P, :], dev[:P, :], dif[:P, :], ALU.add).then_inc(s_var, 1)
            dve.wait_ge(s_root, 1)
            st.link(dve.reciprocal(rstd[:P, :], shift[:P, :]))
            st.mark(dve.scalar_tensor_tensor(shift[:P, :], mean[:P, :], -0.5, rstd[:P, :],
                                             ALU.mult, ALU.mult))

        @block.scalar
        def _(act):
            act.wait_ge(s_var, 1)
            act.activation(shift[:P, :], dev[:P, :], ACT.Sqrt).then_inc(s_root, 1)


def first_stats_phase(nc, g):
    with ExitStack() as ctx:
        block = ctx.enter_context(nc.Block())

        @block.vector
        def _(dve):
            with dve.Fori(0, PAIRS) as i:
                for j in range(2):
                    dve.bn_stats(g.halves[:P, ds(2 * i + j, 1), :], g.X[:P, ds(2 * i + j, 1), :])


def matmul_k(pe, out, lhs, rhs, first=True, last=True):
    ins = None
    for n, (a, b) in enumerate(zip(lhs, rhs)):
        ins = pe.matmul(out, a, b, start=first and n == 0, stop=last and n == len(lhs) - 1)
    return ins


def fold0_phase(nc, g, w):
    with ExitStack() as ctx:
        m = Mem(nc, ctx)
        bvb = m.sb("bvb", [128, 2, 128])
        mean6 = m.sb("mean6", [128, 6])
        pa, pv0, pv1, pb = (m.bank(f"fold0_{n}") for n in range(4))
        s_step, s_bvb, s_mm = m.sem("fold0_step"), m.sem("fold0_bvb"), m.sem("fold0_mm")
        block = ctx.enter_context(nc.Block())

        @block.vector
        def _(dve):
            st = Steps(dve, s_step)
            dve.tensor_copy(bvb[:, :, :], w.bv[:, :].unsqueeze(2).broadcast_to([128, 2, 128])).then_inc(s_bvb, 1)
            st.link(dve.tensor_reduce(mean6[:, :], w.kq[:, :, :], AX, ALU.add))
            st.link(dve.tensor_scalar(mean6[:, :], mean6[:, :], -1.0 / D, None, ALU.mult))
            for n in range(6):
                st.mark(dve.tensor_scalar(w.kq[:, n, :], w.kq[:, n, :], mean6[:, n:n + 1], None, ALU.add))
            st.link(dve.tensor_tensor(w.bsum[:, :], w.b2[:, :], w.bo[:, :], ALU.add))
            dve.wait_ge(s_mm, 1)
            for b in range(2):
                st.mark(dve.tensor_copy(w.cat[:, b, D:D + 16], pa[:, 16 * b:16 * b + 16]))
                st.mark(dve.tensor_copy(w.vo[:, b, :], (pv0, pv1)[b][:, 0:D]))
            st.mark(dve.tensor_copy(w.bvo[:, :], pb[:, 0:D]))
            st.link(dve.tensor_tensor(w.bsum[:, :], w.bsum[:, :], pb[:, 0:D], ALU.add))

        @block.tensor
        def _(pe):
            for b in range(2):
                k = slice(128 * b, 128 * b + 128)
                matmul_k(pe, pa[:, 16 * b:16 * b + 16], [w.WT[:, c, k] for c in range(2)],
                         [w.att[:, c, :] for c in range(2)])
                matmul_k(pe, (pv0, pv1)[b][:, 0:D], [w.vT[:, c, k] for c in range(2)],
                         [w.o[:, c, :] for c in range(2)])
            pe.wait_ge(s_bvb, 1)
            matmul_k(pe, pb[:, 0:D], [bvb[:, c, :] for c in range(2)],
                     [w.o[:, c, :] for c in range(2)]).then_inc(s_mm, 1)


def pass1_phase(nc, g, w, G0, G1):
    with ExitStack() as ctx:
        m = Mem(nc, ctx)
        xn = m.sb("p1_xn", [128, 2, D + 1])
        xnT = m.sb("p1_xnT", [128, 2, 2 * P])
        tab = m.sb("p1_tab", [128, 2, GATW])
        kb = m.sb("p1_kb", [128, 2, D])
        ksq = m.sb("p1_ksq", [128, 2, D])
        k2n = m.sb("p1_k2n", [128, 2, D])
        k4 = m.sb("p1_k4", [128, 2, D])
        ks = m.sb("p1_ks", [128, 2])
        T, K = m.bank("p1_T"), m.bank("p1_K")
        PR = [m.bank(f"p1_P{j}") for j in range(2)]
        G = [G0, G1]
        s_one = m.sem("p1_one")
        s_xn, s_tr, s_xnT, s_proj, s_k = (m.sem(f"p1_{n}") for n in ("xn", "tr", "xnT", "proj", "k"))
        s_tab, s_kb, s_ksq, s_k2n, s_k4, s_sum = (
            m.sem(f"p1_{n}") for n in ("tab", "kb", "ksq", "k2n", "k4", "sum"))
        s_out, s_act, s_dve = m.sem("p1_out"), m.sem("p1_act"), m.sem("p1_dve")
        block = ctx.enter_context(nc.Block())

        @block.gpsimd
        def _(pool):
            pool.memset(xn[:P, :, D:D + 1], 1.0).then_inc(s_one, 1)
            pool.sem_inc(s_out, 16)

        @block.scalar
        def _(act):
            act.wait_ge(s_one, 1)
            with act.Fori(0, PAIRS) as i:
                act.wait_ge(s_sum, i + 1)
                for j in range(2):
                    ins = act.activation(xn[:P, j, 0:D], g.X[:P, ds(2 * i + j, 1), :], ACT.Identity,
                                         bias=g.shift[:P, ds(2 * i + j, 1)], scale=g.rstd[:P, ds(2 * i + j, 1)])
                ins.then_inc(s_xn, 1)
                act.wait_ge(s_proj, i + 1)
                act.wait_ge(s_out, 16 * i + 16)
                for j in range(2):
                    ins = act.activation(tab[:P, j, :], PR[j][:P, 0:GATW], ACT.Identity)
                ins.then_inc(s_tab, 1)
                for j in range(2):
                    act.activation(g.asad[:P, ds(2 * i + j, 1), :], PR[j][:P, D:D + 16].unsqueeze(1),
                                   ACT.Identity)
                act.wait_ge(s_kb, i + 1)
                for j in range(2):
                    ins = act.activation(ksq[:P, j, :], kb[:P, j, :], ACT.Square, accum_out=ks[:P, j:j + 1])
                ins.then_inc(s_ksq, 1)
                act.wait_ge(s_k2n, i + 1)
                act.activation(k4[:P, :, :], k2n[:P, :, :], ACT.Square).then_inc(s_k4, 1)

        @block.vector
        def _(dve):
            with dve.Fori(0, PAIRS) as i:
                st = Steps(dve, s_dve, i * 2)
                dve.wait_ge(s_tr, i + 1)
                dve.tensor_copy(xnT[:, :, :], T[:, 0:4 * P].rearrange("p (b n) -> p b n", b=2)).then_inc(s_xnT, 1)
                dve.wait_ge(s_k, i + 1)
                dve.tensor_tensor(kb[:P, :, :], K[:P, :].rearrange("p (j n) -> p j n", j=2),
                                  w.kq[:P, 2:3, :].broadcast_to([P, 2, D]), ALU.add).then_inc(s_kb, 1)
                dve.wait_ge(s_ksq, i + 1)
                st.link(dve.tensor_scalar(ks[:P, :], ks[:P, :], 1e-7, None, ALU.add))
                st.link(dve.reciprocal(ks[:P, :], ks[:P, :]))
                dve.wait_ge(s_sum, i + 1)
                for j in range(2):
                    ins = dve.tensor_scalar(k2n[:P, j, :], ksq[:P, j, :], ks[:P, j:j + 1], None, ALU.mult)
                ins.then_inc(s_k2n, 1)

        @block.tensor
        def _(pe):
            for b in range(2):
                pe.matmul(G[b][:, :], g.zeros[:, 0:128], g.zeros[:, :], start=True, stop=False)
            pe.sem_inc(s_sum, 1)
            with pe.Fori(0, PAIRS) as i:
                pe.wait_ge(s_xn, i + 1)
                for j in range(2):
                    for b in range(2):
                        ins = pe.transpose(T[:, (2 * b + j) * P:(2 * b + j + 1) * P],
                                           xn[:P, j, 128 * b:128 * b + 128], g.ident[:P, :P])
                ins.then_inc(s_tr, 1)
                pe.wait_ge(s_xnT, i + 1)
                for j in range(2):
                    lhs = [xnT[:, b, j * P:(j + 1) * P] for b in range(2)]
                    ins = matmul_k(pe, K[:P, j * D:(j + 1) * D], lhs, [w.kq[:, b, :] for b in range(2)])
                ins.then_inc(s_k, 1)
                for j in range(2):
                    lhs = [xnT[:, b, j * P:(j + 1) * P] for b in range(2)]
                    ins = matmul_k(pe, PR[j][:P, 0:D + 16], lhs, [w.cat[:, b, :] for b in range(2)])
                ins.then_inc(s_proj, 1)
                pe.wait_ge(s_k4, i + 1)
                for j in range(2):
                    for b in range(2):
                        c = slice(128 * b, 128 * b + 128)
                        pe.matmul(G[b][:, 0:D + 1], k2n[:P, j, c], xn[:P, j, :], start=False, stop=False,
                                  skip_group_check=True)
                        ins = pe.matmul(G[b][:, D + 1:D + 2], k4[:P, j, c], g.ones[:P, 0:1], start=False,
                                        stop=False, skip_group_check=True)
                ins.then_inc(s_sum, 1)
            for b in range(2):
                pe.matmul(G[b][:, :], g.zeros[:, 0:128], g.zeros[:, :], start=False, stop=True)

        @block.sync
        def _(sp):
            with sp.Fori(0, PAIRS) as i:
                sp.wait_ge(s_tab, i + 1)
                sp.dma_start(g.table0.rearrange("(t p) n -> p t n", p=P)[:, ds(2 * i, 2), :],
                             tab[:P, :, :]).then_inc(s_out, 16)
            sp.wait_ge(s_out, 16 * PAIRS + 16)
def ranges_phase(nc, g):
    with ExitStack() as ctx:
        m = Mem(nc, ctx)
        HG = NG // 2
        raw = m.sb("rg_raw", [128, 2, EG], I32)
        dst = m.sb("rg_dst", [128, 2, EG])
        ext = m.sb("rg_ext", [128, 2, 2])
        extb = m.sb("rg_extb", [128, 4, NT])
        tile = m.sb("rg_tile", [128, 2])
        hit = m.sb("rg_hit", [128, NG])
        hit2 = m.sb("rg_hit2", [128, NG])
        a = m.sb("rg_a", [128, NG])
        num = m.sb("rg_num", [128, 3])
        pr, pn = m.bank("rg_pr"), m.bank("rg_pn")
        s_in, s_st, s_ext, s_row, s_num, s_cnt = (m.sem(f"rg_{n}") for n in ("in", "st", "ext", "row", "num", "cnt"))
        block = ctx.enter_context(nc.Block())

        @block.sync
        def _(sp):
            sp.dma_start(raw[:HG, :, :], g.dst_groups).then_inc(s_in, 16)

        @block.vector
        def _(dve):
            st = Steps(dve, s_st)
            st.mark(dve.tensor_scalar(tile[:, 0:1], g.chan[:, :], float(P), None, ALU.mult))
            st.mark(dve.tensor_scalar(tile[:, 1:2], g.chan[:, :], float(P), float(P - 1), ALU.mult, ALU.add))
            dve.wait_ge(s_in, 16)
            st.link(dve.tensor_copy(dst[:HG, :, :], raw[:HG, :, :]))
            st.mark(dve.tensor_reduce(ext[:HG, 0, :], dst[:HG, :, :], AX, ALU.max))
            st.link(dve.tensor_reduce(ext[:HG, 1, :], dst[:HG, :, :], AX, ALU.min))
            dve.tensor_copy(extb[:HG, :, :], ext[:HG, :, :].rearrange("p e a -> p (e a)").unsqueeze(2)
                            .broadcast_to([HG, 4, NT])).then_inc(s_ext, 1)
            dve.wait_ge(s_row, 1)
            st.mark(dve.tensor_scalar(hit[:NT, :], pr[:NT, 0:NG], tile[:NT, 0:1], None, ALU.is_ge))
            st.link(dve.tensor_scalar(hit2[:NT, :], pr[:NT, NG:2 * NG], tile[:NT, 1:2], None, ALU.is_le))
            st.link(dve.tensor_tensor(hit[:NT, :], hit[:NT, :], hit2[:NT, :], ALU.mult))
            st.mark(dve.scalar_tensor_tensor(a[:NT, :], hit[:NT, :], -FAR, g.iota[:NT, 0:NG], ALU.mult, ALU.add))
            st.link(dve.scalar_tensor_tensor(hit2[:NT, :], g.iota[:NT, 0:NG], 1.0, hit[:NT, :], ALU.add, ALU.mult))
            st.mark(dve.tensor_reduce(num[:NT, 0:1], a[:NT, :], AX, ALU.min))
            st.link(dve.tensor_reduce(num[:NT, 1:2], hit2[:NT, :], AX, ALU.max))
            st.link(dve.tensor_scalar(num[:NT, 0:1], num[:NT, 0:1], FAR, float(NG - 1), ALU.add, ALU.min))
            st.link(dve.tensor_tensor(num[:NT, 2:3], num[:NT, 1:2], num[:NT, 0:1], ALU.subtract))
            dve.tensor_scalar(num[:NT, 2:3], num[:NT, 2:3], 1.0, None, ALU.max).then_inc(s_num, 1)
            dve.wait_ge(s_cnt, 1)
            dve.tensor_copy(g.visits[0:1, :, :], pn[0:1, 0:3 * NT].rearrange("p (a t) -> p t a", a=3))

        @block.tensor
        def _(pe):
            pe.wait_ge(s_ext, 1)
            for n in range(4):
                c = (n // 2) * NG + (n % 2) * HG
                ins = pe.matmul(pr[:NT, c:c + HG], extb[:HG, n, :], g.ident[:HG, :HG], start=True, stop=True)
            ins.then_inc(s_row, 1)
            pe.wait_ge(s_num, 1)
            pe.matmul(pn[0:1, 0:NT], num[:NT, 0:1], g.ident[:NT, :NT], start=True, stop=True)
            pe.matmul(pn[0:1, NT:2 * NT], num[:NT, 2:3], g.ident[:NT, :NT], start=True, stop=True)
            pe.matmul(pn[0:1, 2 * NT:3 * NT], num[:NT, 2:3], g.before[:NT, :], start=True, stop=True)\
              .then_inc(s_cnt, 1)


def edge_lists_phase(nc, g):
    with ExitStack() as ctx:
        m = Mem(nc, ctx)
        block = ctx.enter_context(nc.Block())

        @block.vector
        def _(dve):
            dve.tensor_copy(g.dst[:P, :], g.dst_i[:P, :])
            dve.tensor_copy(g.rel[:P, :], g.rel_i[:P, :])


def visit_range(eng, g, t):
    v = g.visits[0:1, ds(t, 1), :]
    lo = eng.value_load(v[:, :, 0:1], min_val=0, max_val=NG - 1)
    n = eng.value_load(v[:, :, 1:2], min_val=1, max_val=NG)
    done = eng.value_load(v[:, :, 2:3], min_val=0, max_val=NG * NT)
    return lo, n, done


def group(eng, lo, j):
    return eng.bass.s_assert_within(
        lo + j, 0, NG - 1,
        skip_runtime_bounds_check_because="lo + n <= NG by ranges_phase, and j < n")


def gather_visits(pool, g, table, width, out, idx, s_idx, s_taken, s_free, s_gath):
    with pool.Fori(0, NT) as t:
        lo, n, done = visit_range(pool, g, t)
        with pool.Fori(0, n) as j:
            v = done + j + 1
            for a in range(2):
                pool.wait_ge(s_free[a], v)
                pool.tensor_copy(idx[a][:P, :], g.src_i[:P, ds(ET * group(pool, lo, j) + a * HT, HT)])\
                    .then_inc(s_idx[a], 1)
                pool.wait_ge(s_idx[a], v)
                pool.sem_inc(s_taken, 1)
                for k in range(HT):
                    pool.indirect_dma_start(out[a][:P, k, 0:width], None, table,
                                            bass.IndirectOffsetOnAxis(idx[a][:P, k:k + 1], 0))\
                        .then_inc(s_gath[a], 16)


def attend_edges_phase(nc, g, w):
    with ExitStack() as ctx:
        m = Mem(nc, ctx)
        two = range(2)
        rows_ = [m.sb(f"ga_rows{a}", [128, HT, GATW]) for a in two]
        msg = [m.sb(f"ga_msg{a}", [128, HT, GATW]) for a in two]
        hot = [m.sb(f"ga_hot{a}", [128, HT, P]) for a in two]
        hotT = [m.sb(f"ga_hotT{a}", [128, HT, P]) for a in two]
        loc = [m.sb(f"ga_loc{a}", [128, HT]) for a in two]
        sc = [m.sb(f"ga_sc{a}", [128, HT, H]) for a in two]
        sc2 = [m.sb(f"ga_sc2{a}", [128, HT, H]) for a in two]
        idx = [m.sb(f"ga_idx{a}", [128, HT], I32) for a in two]
        xn = m.sb("ga_xn", [128, D])
        den = m.sb("ga_den", [128, H])
        r = m.sb("ga_r", [128, D])
        tdst = m.sb("ga_tdst", [128, 16])
        own = m.sb("ga_own", [128, GATW])
        ptr = [m.bank(f"ga_ptr{a}") for a in two]
        pdst = [m.bank(f"ga_pdst{a}") for a in two]
        acc = m.bank("ga_acc")
        names = ("acc", "fin", "xn", "tdst", "vst", "tst", "own", "done", "taken")
        s = {n: m.sem(f"ga_{n}") for n in names}
        per_half = ("gath", "idx", "free", "hot", "turned", "hotT", "dst", "sc", "exp", "msg", "sum")
        h = {n: [m.sem(f"ga_{n}{a}") for a in two] for n in per_half}
        block = ctx.enter_context(nc.Block())

        @block.sync
        def _(sp):
            sp.sem_inc(s["done"], 1)
            with sp.Fori(0, NT) as t:
                sp.wait_ge(s["done"], t + 1)
                sp.dma_start(own[:P, :], g.table0[ds(P * t, P), :]).then_inc(s["own"], 16)

        @block.gpsimd
        def _(pool):
            gather_visits(pool, g, g.table0, GATW, rows_, idx, h["idx"], s["taken"], h["free"], h["gath"])

        @block.vector
        def _(dve):
            for a in two:
                dve.sem_inc(h["free"][a], 1)
            with dve.Fori(0, NT) as t:
                lo, n, done = visit_range(dve, g, t)
                with dve.Fori(0, n) as j:
                    v = done + j + 1
                    vst = Steps(dve, s["vst"], (done + j) * 6)

                    for a in two:
                        vst.link(dve.tensor_scalar(loc[a][:P, :], g.dst[:P, ds(ET * group(dve, lo, j) + a * HT, HT)],
                                                   g.tile0[:P, ds(t, 1)], None, ALU.subtract))
                        dve.wait_ge(h["sum"][a], v)
                        dve.tensor_tensor(hot[a][:P, :, :], g.iota[:P, 0:P].unsqueeze(1).broadcast_to([P, HT, P]),
                                          loc[a][:P, :].unsqueeze(2).broadcast_to([P, HT, P]), ALU.is_equal)\
                           .then_inc(h["hot"][a], 1)
                    for a in two:
                        dve.wait_ge(h["gath"][a], 16 * HT * v)
                        dve.wait_ge(h["dst"][a], v)
                        pd = pdst[a][:P, 0:16 * HT].rearrange("p (k n) -> p k n", k=HT)
                        vst.link(dve.tensor_tensor(sc[a][:P, :, :], rows_[a][:P, :, D:GATW], pd[:, :, 0:H], ALU.add))
                        vst.link(dve.scalar_tensor_tensor(sc2[a][:P, :, :], sc[a][:P, :, :], 0.2, sc[a][:P, :, :],
                                                          ALU.mult, ALU.max))
                        dve.tensor_tensor(sc[a][:P, :, :], sc2[a][:P, :, :], pd[:, :, H:2 * H], ALU.subtract)\
                           .then_inc(h["sc"][a], 1)
                        dve.wait_ge(h["exp"][a], v)
                        for k in range(HT):
                            ins = dve.tensor_tensor(
                                msg[a][:P, k, 0:D].rearrange("p (h c) -> p h c", h=H),
                                rows_[a][:P, k, 0:D].rearrange("p (h c) -> p h c", h=H),
                                msg[a][:P, k, D:GATW].unsqueeze(2).broadcast_to([P, H, HD]), ALU.mult)
                        ins.then_inc(h["msg"][a], 1)
                        dve.wait_ge(h["msg"][a], v)
                        dve.sem_inc(h["free"][a], 1)
                heads = lambda x: x.rearrange("p (h c) -> p h c", h=H)
                tst = Steps(dve, s["tst"], t * 7)
                wself = g.wself[:P, ds(t, 1), :].rearrange("p t h -> p (t h)")
                dve.wait_ge(s["own"], 16 * t + 16)
                tst.mark(dve.tensor_tensor(heads(r[:P, :]), heads(own[:P, 0:D]),
                                           wself.unsqueeze(2).broadcast_to([P, H, HD]), ALU.mult))
                dve.wait_ge(s["acc"], t + 1)
                tst.link(dve.scalar_tensor_tensor(den[:P, :], acc[:P, D:GATW], 1e-16, wself, ALU.add, ALU.add))
                tst.mark(dve.tensor_tensor(r[:P, :], r[:P, :], acc[:P, 0:D], ALU.add))
                tst.link(dve.reciprocal(den[:P, :], den[:P, :]))
                tst.link(dve.tensor_tensor(heads(r[:P, :]), heads(r[:P, :]),
                                           den[:P, :].unsqueeze(2).broadcast_to([P, H, HD]), ALU.mult))
                tst.link(dve.tensor_tensor(r[:P, :], r[:P, :], w.gbias[:P, :], ALU.add))
                dve.wait_ge(s["xn"], t + 1)
                tst.link(dve.tensor_tensor(g.R[:P, ds(t, 1), :], r[:P, :].unsqueeze(1),
                                           xn[:P, :].unsqueeze(1), ALU.add))
                dve.bn_stats(g.rhalves[:P, ds(t, 1), :], g.R[:P, ds(t, 1), :]).then_inc(s["fin"], 1)
                dve.wait_ge(s["fin"], t + 2)
                dve.sem_inc(s["done"], 1)

        @block.scalar
        def _(act):
            act.sem_inc(s["fin"], 1)
            with act.Fori(0, NT) as t:
                lo, n, done = visit_range(act, g, t)
                act.wait_ge(s["fin"], t + 1)
                act.activation(tdst[:P, :], g.tdst[:P, ds(t, 1), :], ACT.Identity).then_inc(s["tdst"], 1)
                act.activation(xn[:P, :], g.X[:P, ds(t, 1), :], ACT.Identity, bias=g.shift[:P, ds(t, 1)],
                               scale=g.rstd[:P, ds(t, 1)]).then_inc(s["xn"], 1)
                with act.Fori(0, n) as j:
                    v = done + j + 1
                    for a in two:
                        act.wait_ge(h["turned"][a], v)
                        act.activation(hotT[a][:P, :, :], ptr[a][:P, 0:HT * P].rearrange("p (k e) -> p k e", k=HT),
                                       ACT.Identity).then_inc(h["hotT"][a], 1)
                    for a in two:
                        act.wait_ge(h["sc"][a], v)
                        act.activation(msg[a][:P, :, D:GATW], sc[a][:P, :, :], ACT.Exp).then_inc(h["exp"][a], 1)

        @block.tensor
        def _(pe):
            for a in two:
                pe.sem_inc(h["sum"][a], 1)
            with pe.Fori(0, NT) as t:
                lo, n, done = visit_range(pe, g, t)
                pe.wait_ge(s["fin"], t + 1)
                pe.wait_ge(s["tdst"], t + 1)
                pe.matmul(acc[:, :], g.zeros[:, 0:128], g.zeros[:, :], start=True, stop=False)
                with pe.Fori(0, n) as j:
                    v = done + j + 1
                    for a in two:
                        pe.wait_ge(h["hot"][a], v)
                        for k in range(HT):
                            ins = pe.transpose(ptr[a][:P, k * P:(k + 1) * P], hot[a][:P, k, :], g.ident[:P, :P])
                        ins.then_inc(h["turned"][a], 1)
                    for a in two:
                        pe.wait_ge(h["hotT"][a], v)
                        for k in range(HT):
                            ins = pe.matmul(pdst[a][:P, 16 * k:16 * k + 16], hotT[a][:P, k, :], tdst[:P, :],
                                            start=True, stop=True)
                        ins.then_inc(h["dst"][a], 1)
                    for a in two:
                        pe.wait_ge(h["msg"][a], v)
                        for k in range(HT):
                            ins = pe.matmul(acc[:P, 0:GATW], hot[a][:P, k, :], msg[a][:P, k, :], start=False,
                                            stop=False, skip_group_check=True)
                        ins.then_inc(h["sum"][a], 1)
                pe.matmul(acc[:, :], g.zeros[:, 0:128], g.zeros[:, :], start=False, stop=True)\
                  .then_inc(s["acc"], 1)


def guard_phase(nc, g):
    with ExitStack() as ctx:
        m = Mem(nc, ctx)
        top = m.sb("gu_top", [128, H])
        topT = m.sb("gu_topT", [128, 1])
        topb = m.sb("gu_topb", [128, P])
        bound, bound2, own, own2 = (m.sb(f"gu_{n}", [128, NT, H]) for n in ("bound", "bound2", "own", "own2"))
        pt, pb = m.bank("gu_pt"), m.bank("gu_pb")
        s_st, s_top, s_t, s_topb, s_b, s_own = (m.sem(f"gu_{n}") for n in ("st", "top", "t", "topb", "b", "own"))
        block = ctx.enter_context(nc.Block())
        a_src, a_dst = g.asad[:P, :, 0:H], g.asad[:P, :, H:2 * H]

        @block.vector
        def _(dve):
            st = Steps(dve, s_st)
            dve.tensor_reduce(top[:P, :], a_src.rearrange("p t h -> p h t"), AX, ALU.max).then_inc(s_top, 1)
            dve.wait_ge(s_t, 1)
            st.link(dve.tensor_reduce(topT[:H, :], pt[:H, 0:P], AX, ALU.max))
            dve.tensor_copy(topb[:H, :], topT[:H, :].broadcast_to([H, P])).then_inc(s_topb, 1)
            dve.wait_ge(s_b, 1)
            st.mark(dve.tensor_tensor(own[:P, :, :], a_src, a_dst, ALU.add))
            st.link(dve.tensor_tensor(bound[:P, :, :], a_dst, pb[:P, 0:H].unsqueeze(1).broadcast_to([P, NT, H]),
                                      ALU.add))
            st.mark(dve.scalar_tensor_tensor(bound2[:P, :, :], bound[:P, :, :], 0.2, bound[:P, :, :],
                                             ALU.mult, ALU.max))
            st.link(dve.scalar_tensor_tensor(own2[:P, :, :], own[:P, :, :], 0.2, own[:P, :, :],
                                             ALU.mult, ALU.max))
            st.link(dve.scalar_tensor_tensor(g.tdst[:P, :, H:2 * H], bound2[:P, :, :], -GUARD, own2[:P, :, :],
                                             ALU.add, ALU.max))
            dve.tensor_tensor(own[:P, :, :], own2[:P, :, :], g.tdst[:P, :, H:2 * H], ALU.subtract)\
               .then_inc(s_own, 1)
            dve.tensor_copy(g.tdst[:P, :, 0:H], a_dst)

        @block.scalar
        def _(act):
            act.wait_ge(s_own, 1)
            act.activation(g.wself[:P, :, :], own[:P, :, :], ACT.Exp)

        @block.tensor
        def _(pe):
            pe.wait_ge(s_top, 1)
            pe.transpose(pt[:H, 0:P], top[:P, :], g.ident[:P, :P]).then_inc(s_t, 1)
            pe.wait_ge(s_topb, 1)
            pe.matmul(pb[:P, 0:H], topb[:H, :], g.ident[:H, :H], start=True, stop=True).then_inc(s_b, 1)


def relation_edges_phase(nc, g):
    with ExitStack() as ctx:
        m = Mem(nc, ctx)
        two = range(2)
        rows_ = [m.sb(f"ge_rows{a}", [128, HT, RELW]) for a in two]
        hot = [m.sb(f"ge_hot{a}", [128, HT, P]) for a in two]
        loc = [m.sb(f"ge_loc{a}", [128, HT]) for a in two]
        idx = [m.sb(f"ge_idx{a}", [128, HT], I32) for a in two]
        acc = m.bank("ge_acc")
        s = {n: m.sem(f"ge_{n}") for n in ("acc", "fin", "vst", "taken")}
        h = {n: [m.sem(f"ge_{n}{a}") for a in two] for n in ("gath", "idx", "free", "hot")}
        block = ctx.enter_context(nc.Block())

        @block.gpsimd
        def _(pool):
            gather_visits(pool, g, g.table1, D, rows_, idx, h["idx"], s["taken"], h["free"], h["gath"])

        @block.vector
        def _(dve):
            dve.sem_inc(s["fin"], 1)
            with dve.Fori(0, NT) as t:
                lo, n, done = visit_range(dve, g, t)
                with dve.Fori(0, n) as j:
                    v = done + j + 1
                    vst = Steps(dve, s["vst"], (done + j) * 2)
                    for a in two:
                        at = ds(ET * group(dve, lo, j) + a * HT, HT)
                        vst.link(dve.tensor_scalar(loc[a][:P, :], g.dst[:P, at], g.tile0[:P, ds(t, 1)], None,
                                                   ALU.subtract))
                        dve.wait_ge(h["free"][a], v)
                        dve.tensor_tensor(rows_[a][:P, :, D:RELW],
                                          g.iota[:P, 0:NREL].unsqueeze(1).broadcast_to([P, HT, NREL]),
                                          g.rel[:P, at].unsqueeze(2).broadcast_to([P, HT, NREL]), ALU.is_equal)
                        dve.tensor_tensor(hot[a][:P, :, :], g.iota[:P, 0:P].unsqueeze(1).broadcast_to([P, HT, P]),
                                          loc[a][:P, :].unsqueeze(2).broadcast_to([P, HT, P]), ALU.is_equal)\
                           .then_inc(h["hot"][a], 1)
                dve.wait_ge(s["acc"], t + 1)
                dve.tensor_copy(g.red[:P, ds(t, 1), :], acc[:P, 0:RELW].unsqueeze(1)).then_inc(s["fin"], 1)

        @block.tensor
        def _(pe):
            for a in two:
                pe.sem_inc(h["free"][a], 1)
            with pe.Fori(0, NT) as t:
                lo, n, done = visit_range(pe, g, t)
                pe.wait_ge(s["fin"], t + 1)
                pe.matmul(acc[:, :], g.zeros[:, 0:128], g.zeros[:, :], start=True, stop=False)
                with pe.Fori(0, n) as j:
                    v = done + j + 1
                    for a in two:
                        pe.wait_ge(h["hot"][a], v)
                        pe.wait_ge(h["gath"][a], 16 * HT * v)
                        for k in range(HT):
                            ins = pe.matmul(acc[:P, 0:RELW], hot[a][:P, k, :], rows_[a][:P, k, :], start=False,
                                            stop=False, skip_group_check=True)
                        ins.then_inc(h["free"][a], 1)
                pe.matmul(acc[:, :], g.zeros[:, 0:128], g.zeros[:, :], start=False, stop=True)\
                  .then_inc(s["acc"], 1)
def normalise(act, g, src, out, i, rstd, shift):
    ins = None
    for j in range(2):
        ins = act.activation(out[:P, j, 0:D], src[:P, ds(2 * i + j, 1), :], ACT.Identity,
                             bias=shift[:P, ds(2 * i + j, 1)], scale=rstd[:P, ds(2 * i + j, 1)])
    return ins


def turn_pair(pe, g, bank, src, blocks=2):
    ins = None
    for j in range(2):
        for b in range(blocks):
            ins = pe.transpose(bank[:, (2 * b + j) * P:(2 * b + j + 1) * P], src[:P, j, 128 * b:128 * b + 128],
                               g.ident[:P, :P])
    return ins


def pair_blocks(bank, blocks=2):
    return bank[:, 0:2 * P * blocks].rearrange("p (b n) -> p b n", b=blocks)


def tile_of(xT, j):
    return [xT[:, b, j * P:(j + 1) * P] for b in range(2)]


def mixer0_fold_phase(nc, g, w, G0, G1):
    with ExitStack() as ctx:
        m = Mem(nc, ctx)
        norm = m.sb("mf_norm", [128, 2])
        Gs = m.sb("mf_G", [128, 2, D + 1])
        GT = m.sb("mf_GT", [128, 2, D])
        sT = m.sb("mf_sT", [1, D])
        pt, ps, po = m.bank("mf_pt"), m.bank("mf_ps"), m.bank("mf_po")
        s_st, s_nrm, s_root, s_G, s_t, s_GT, s_o = (
            m.sem(f"mf_{n}") for n in ("st", "nrm", "root", "G", "t", "GT", "o"))
        block = ctx.enter_context(nc.Block())

        @block.vector
        def _(dve):
            st = Steps(dve, s_st)
            for b, G in enumerate((G0, G1)):
                ins = dve.tensor_copy(norm[:, b:b + 1], G[:, D + 1:D + 2])
            ins.then_inc(s_nrm, 1)
            dve.wait_ge(s_root, 1)
            st.link(dve.tensor_scalar(norm[:, :], norm[:, :], 1e-12, float(np.sqrt(N)), ALU.max, ALU.mult))
            st.link(dve.reciprocal(norm[:, :], norm[:, :]))
            for b, G in enumerate((G0, G1)):
                ins = dve.tensor_scalar(Gs[:, b, :], G[:, 0:D + 1], norm[:, b:b + 1], None, ALU.mult)
            ins.then_inc(s_G, 1)
            dve.wait_ge(s_t, 1)
            dve.tensor_copy(GT[:, :, :], pt[:, :].rearrange("p (b n) -> p b n", b=2))
            dve.tensor_copy(sT[:, :], ps[0:1, 0:D]).then_inc(s_GT, 1)
            dve.wait_ge(s_o, 1)
            dve.tensor_copy(w.mwo[:, :, :], po[:, :].rearrange("p (b n) -> p b n", b=2))

        @block.scalar
        def _(act):
            act.wait_ge(s_nrm, 1)
            act.activation(norm[:, :], norm[:, :], ACT.Sqrt).then_inc(s_root, 1)

        @block.tensor
        def _(pe):
            pe.wait_ge(s_G, 1)
            for c in range(2):
                for k in range(2):
                    pe.transpose(pt[:, k * D + c * 128:k * D + c * 128 + 128], Gs[:, c, 128 * k:128 * k + 128],
                                 g.ident[:, :])
                ins = pe.transpose(ps[0:1, 128 * c:128 * c + 128], Gs[:, c, D:D + 1], g.ident[:, :])
            ins.then_inc(s_t, 1)
            pe.wait_ge(s_GT, 1)
            for c in range(2):
                r = slice(128 * c, 128 * c + 128)
                ins = matmul_k(pe, po[:, c * D:(c + 1) * D], [GT[:, 0, r], GT[:, 1, r], sT[:, r]],
                               [w.vo[:, 0, :], w.vo[:, 1, :], w.bvo[0:1, :]])
            ins.then_inc(s_o, 1)


def layer0_dense_phase(nc, g, w):
    with ExitStack() as ctx:
        m = Mem(nc, ctx)
        rn = m.sb("l0_rn", [128, 2, D])
        xn = m.sb("l0_xn", [128, 2, D])
        rnT, xnT, zs, q2T = (m.sb(f"l0_{n}", [128, 2, 2 * P]) for n in ("rnT", "xnT", "zs", "q2T"))
        qb, qsq, junk, q2 = (m.sb(f"l0_{n}", [128, 2, D]) for n in ("qb", "qsq", "junk", "q2"))
        qs, q4s, root = (m.sb(f"l0_{n}", [128, 2]) for n in ("qs", "q4s", "root"))
        y = m.sb("l0_y", [128, 2, D])
        TR, TX, Z, Q, TQ, Y = (m.bank(f"l0_{n}") for n in ("TR", "TX", "Z", "Q", "TQ", "Y"))
        names = ("rn", "xn", "trn", "txn", "rnT", "xnT", "z", "q", "zs", "qb", "qsq", "root", "q2", "tq", "q2T",
                 "y", "free", "st", "ast")
        s = {n: m.sem(f"l0_{n}") for n in names}
        block = ctx.enter_context(nc.Block())

        @block.scalar
        def _(act):
            with act.Fori(0, PAIRS) as i:
                v = i + 1
                ast = Steps(act, s["ast"], i)
                normalise(act, g, g.R, rn, i, g.rrstd, g.rshift).then_inc(s["rn"], 1)
                normalise(act, g, g.X, xn, i, g.rstd, g.shift).then_inc(s["xn"], 1)
                act.wait_ge(s["trn"], v)
                for b in range(2):
                    ins = act.activation(rnT[:, b, :], pair_blocks(TR)[:, b, :], ACT.Identity,
                                         bias=w.lnb[:, b:b + 1], scale=w.lng[:, b:b + 1])
                ins.then_inc(s["rnT"], 1)
                act.wait_ge(s["z"], v)
                for b in range(2):
                    ins = act.activation(zs[:, b, :], pair_blocks(Z)[:, b, :], ACT.Relu, bias=w.b1[:, b:b + 1])
                ins.then_inc(s["zs"], 1)
                act.wait_ge(s["qb"], v)
                for j in range(2):
                    ins = act.activation(qsq[:P, j, :], qb[:P, j, :], ACT.Square, accum_out=qs[:P, j:j + 1])
                ast.link(ins)
                for j in range(2):
                    act.activation(junk[:P, j, :], qsq[:P, j, :], ACT.Square, accum_out=q4s[:P, j:j + 1])\
                       .then_inc(s["qsq"], 1)
                act.wait_ge(s["qsq"], 2 * v)
                act.activation(root[:P, :], q4s[:P, :], ACT.Sqrt).then_inc(s["root"], 1)
                act.wait_ge(s["tq"], v)
                act.activation(q2T[:, :, :], pair_blocks(TQ), ACT.Identity).then_inc(s["q2T"], 1)
                act.wait_ge(s["y"], v)

        @block.vector
        def _(dve):
            with dve.Fori(0, PAIRS) as i:
                v = i + 1
                st = Steps(dve, s["st"], i * 8)
                dve.wait_ge(s["txn"], v)
                dve.tensor_copy(xnT[:, :, :], pair_blocks(TX)).then_inc(s["xnT"], 1)
                dve.wait_ge(s["q"], v)
                dve.tensor_tensor(qb[:P, :, :], Q[:P, :].rearrange("p (j n) -> p j n", j=2),
                                  w.kq[:P, 5:6, :].broadcast_to([P, 2, D]), ALU.add).then_inc(s["qb"], 1)
                dve.wait_ge(s["root"], v)
                st.link(dve.tensor_scalar(qs[:P, :], qs[:P, :], 1e-7, None, ALU.add))
                st.link(dve.reciprocal(qs[:P, :], qs[:P, :]))
                st.link(dve.tensor_tensor(root[:P, :], root[:P, :], qs[:P, :], ALU.mult))
                st.link(dve.tensor_scalar(root[:P, :], root[:P, :], 1e-12, None, ALU.max))
                st.link(dve.reciprocal(root[:P, :], root[:P, :]))
                st.link(dve.tensor_tensor(root[:P, :], root[:P, :], qs[:P, :], ALU.mult))
                for j in range(2):
                    ins = dve.tensor_scalar(q2[:P, j, :], qsq[:P, j, :], root[:P, j:j + 1], None, ALU.mult)
                ins.then_inc(s["q2"], 1)
                dve.wait_ge(s["y"], v)
                st.link(dve.tensor_tensor(y[:P, :, :], Y[:P, :].rearrange("p (j n) -> p j n", j=2),
                                          w.bsum[:P, :].unsqueeze(1).broadcast_to([P, 2, D]), ALU.add))
                st.link(dve.tensor_tensor(g.X[:P, ds(2 * i, 2), :], y[:P, :, :], g.X[:P, ds(2 * i, 2), :], ALU.add))
                for j in range(2):
                    dve.bn_stats(g.halves[:P, ds(2 * i + j, 1), :], g.X[:P, ds(2 * i + j, 1), :])

        @block.tensor
        def _(pe):
            with pe.Fori(0, PAIRS) as i:
                v = i + 1
                pe.wait_ge(s["rn"], v)
                turn_pair(pe, g, TR, rn).then_inc(s["trn"], 1)
                pe.wait_ge(s["xn"], v)
                turn_pair(pe, g, TX, xn).then_inc(s["txn"], 1)
                pe.wait_ge(s["rnT"], v)
                for c in range(2):
                    ins = matmul_k(pe, Z[:, c * 2 * P:(c + 1) * 2 * P],
                                   [w.w1[:, b, 128 * c:128 * c + 128] for b in range(2)],
                                   [rnT[:, b, :] for b in range(2)])
                ins.then_inc(s["z"], 1)
                pe.wait_ge(s["xnT"], v)
                for j in range(2):
                    ins = matmul_k(pe, Q[:P, j * D:(j + 1) * D], tile_of(xnT, j), [w.kq[:, 3 + b, :] for b in range(2)])
                ins.then_inc(s["q"], 1)
                pe.wait_ge(s["q2"], v)
                turn_pair(pe, g, TQ, q2).then_inc(s["tq"], 1)
                pe.wait_ge(s["zs"], v)
                pe.wait_ge(s["q2T"], v)
                for j in range(2):
                    ins = matmul_k(pe, Y[:P, j * D:(j + 1) * D], tile_of(zs, j) + tile_of(xnT, j) + tile_of(q2T, j),
                                   [wt[:, b, :] for wt in (w.w2, w.vo, w.mwo) for b in range(2)])
                ins.then_inc(s["y"], 1)


def fold_slices_phase(nc, g, w):
    with ExitStack() as ctx:
        m = Mem(nc, ctx)
        bxb = m.sb("fs_bxb", [128, 4, 128])
        PL = [m.bank(f"fs_L{b}") for b in range(2)]
        PB = m.bank("fs_B")
        s_st, s_bx, s_mm = (m.sem(f"fs_{n}") for n in ("st", "bx", "mm"))
        block = ctx.enter_context(nc.Block())
        per_slice = lambda a: a.rearrange("p (h s) -> p h s", h=H)
        temp = w.temp[:, :].unsqueeze(2).broadcast_to([128, H, S])

        @block.vector
        def _(dve):
            st = Steps(dve, s_st)
            dve.tensor_copy(bxb[:, :, :], w.bx[:, :].unsqueeze(2).broadcast_to([128, 4, 128])).then_inc(s_bx, 1)
            st.link(dve.tensor_scalar(w.temp[:, :], w.temp[:, :], 0.1, 5.0, ALU.max, ALU.min))
            st.link(dve.reciprocal(w.temp[:, :], w.temp[:, :]))
            dve.wait_ge(s_mm, 1)
            for b in range(2):
                dve.tensor_tensor(per_slice(w.lg[:, b, :]), per_slice(PL[b][:, :]), temp, ALU.mult)
            st.link(dve.tensor_tensor(per_slice(w.lb[:, :]), per_slice(PB[:, :]),
                                      w.bs[:, :].unsqueeze(1).broadcast_to([128, H, S]), ALU.add))
            st.link(dve.tensor_tensor(per_slice(w.lb[:, :]), per_slice(w.lb[:, :]), temp, ALU.mult))

        @block.tensor
        def _(pe):
            for b in range(2):
                for c in range(4):
                    pe.matmul(PL[b][:, 128 * c:128 * c + 128], w.xT[:, c, 128 * b:128 * b + 128], w.ws2[:, :],
                              start=True, stop=True)
            pe.wait_ge(s_bx, 1)
            for c in range(4):
                ins = pe.matmul(PB[:, 128 * c:128 * c + 128], bxb[:, c, :], w.ws2[:, :], start=True, stop=True)
            ins.then_inc(s_mm, 1)


def slice_sums_phase(nc, g, w, SL):
    with ExitStack() as ctx:
        m = Mem(nc, ctx)
        xn = m.sb("ss_xn", [128, 2, D + 1])
        xnT = m.sb("ss_xnT", [128, 2, 2 * P])
        lo = m.sb("ss_lo", [128, 2, 8 * S])
        top = m.sb("ss_top", [128, 2, H])
        tot = m.sb("ss_tot", [128, 2, H])
        T = m.bank("ss_T")
        L = [m.bank(f"ss_L{j}") for j in range(2)]
        names = ("one", "xn", "tr", "xnT", "log", "exp", "w", "sum", "st", "kept")
        s = {n: m.sem(f"ss_{n}") for n in names}
        s_lo = [m.sem(f"ss_lo{j}") for j in range(2)]
        block = ctx.enter_context(nc.Block())
        hs = lambda a: a.rearrange("p (h s) -> p h s", h=H)

        @block.gpsimd
        def _(pool):
            pool.memset(xn[:P, :, D:D + 1], 1.0).then_inc(s["one"], 1)
            pool.sem_inc(s["kept"], 1)
            with pool.Fori(0, PAIRS) as i:
                pool.wait_ge(s["w"], 2 * i + 2)
                pool.tensor_copy(g.W[:P, ds(2 * i, 2), :], lo[:P, :, :]).then_inc(s["kept"], 1)

        @block.scalar
        def _(act):
            act.wait_ge(s["one"], 1)
            with act.Fori(0, PAIRS) as i:
                v = i + 1
                act.wait_ge(s["sum"], v)
                normalise(act, g, g.X, xn, i, g.rstd, g.shift).then_inc(s["xn"], 1)
                for j in range(2):
                    act.wait_ge(s_lo[j], v)
                    act.activation(lo[:P, j, :], lo[:P, j, :], ACT.Exp).then_inc(s["exp"], 1)

        @block.vector
        def _(dve):
            with dve.Fori(0, PAIRS) as i:
                v = i + 1
                st = Steps(dve, s["st"], i * 8)
                dve.wait_ge(s["tr"], v)
                dve.tensor_copy(xnT[:, :, :], pair_blocks(T)).then_inc(s["xnT"], 1)
                dve.wait_ge(s["log"], v)
                dve.wait_ge(s["kept"], v)
                for j in range(2):
                    st.mark(dve.tensor_tensor(lo[:P, j, :], L[j][:P, :], w.lb[:P, :], ALU.add))
                st.wait()
                for j in range(2):
                    st.link(dve.tensor_reduce(top[:P, j, :], hs(lo[:P, j, :]), AX, ALU.max))
                    dve.tensor_tensor(hs(lo[:P, j, :]), hs(lo[:P, j, :]),
                                      top[:P, j, :].unsqueeze(2).broadcast_to([P, H, S]), ALU.subtract)\
                       .then_inc(s_lo[j], 1)
                for j in range(2):
                    dve.wait_ge(s["exp"], 2 * i + j + 1)
                    st.link(dve.tensor_reduce(tot[:P, j, :], hs(lo[:P, j, :]), AX, ALU.add))
                    st.link(dve.reciprocal(tot[:P, j, :], tot[:P, j, :]))
                    dve.tensor_tensor(hs(lo[:P, j, :]), hs(lo[:P, j, :]),
                                      tot[:P, j, :].unsqueeze(2).broadcast_to([P, H, S]), ALU.mult)\
                       .then_inc(s["w"], 1)

        @block.tensor
        def _(pe):
            for b in range(4):
                pe.matmul(SL[b][:, :], g.zeros[:, 0:128], g.zeros[:, :], start=True, stop=False)
            pe.sem_inc(s["sum"], 1)
            with pe.Fori(0, PAIRS) as i:
                v = i + 1
                pe.wait_ge(s["xn"], v)
                turn_pair(pe, g, T, xn).then_inc(s["tr"], 1)
                pe.wait_ge(s["xnT"], v)
                for j in range(2):
                    ins = matmul_k(pe, L[j][:P, :], tile_of(xnT, j), [w.lg[:, b, :] for b in range(2)])
                ins.then_inc(s["log"], 1)
                pe.wait_ge(s["w"], 2 * v)
                for j in range(2):
                    for b in range(4):
                        ins = pe.matmul(SL[b][:, 0:D + 1], lo[:P, j, 128 * b:128 * b + 128], xn[:P, j, :],
                                        start=False, stop=False, skip_group_check=True)
                ins.then_inc(s["sum"], 1)
            for b in range(4):
                pe.matmul(SL[b][:, :], g.zeros[:, 0:128], g.zeros[:, :], start=False, stop=True)


def slice_attention_phase(nc, g, w, SL):
    with ExitStack() as ctx:
        m = Mem(nc, ctx)
        inv = m.sb("sa_inv", [128, 4])
        A = m.sb("sa_A", [128, 4, D + 1])
        AT = m.sb("sa_AT", [128, 2, 512])
        nT = m.sb("sa_nT", [1, 512])
        TT, qT, kT, v_, at = (m.sb(f"sa_{n}", [S, 512]) for n in ("TT", "qT", "kT", "v", "at"))
        atT, oT = qT, TT
        top = m.sb("sa_top", [S, H])
        s_st, s_pe, s_act, s_out = (m.sem(f"sa_{n}") for n in ("st", "pe", "act", "out"))
        with ExitStack() as c1:
            m1 = Mem(nc, c1)
            block = c1.enter_context(nc.Block(name="sa_scale"))

            @block.vector
            def _(dve):
                st = Steps(dve, s_st)
                for b in range(4):
                    st.mark(dve.tensor_scalar(inv[:, b:b + 1], SL[b][:, D:D + 1], 1e-5, None, ALU.add))
                st.wait()
                st.link(dve.reciprocal(inv[:, :], inv[:, :]))
                for b in range(4):
                    dve.tensor_scalar(A[:, b, :], SL[b][:, 0:D + 1], inv[:, b:b + 1], None, ALU.mult)
        B0, B1, B2, B3 = SL
        with ExitStack() as c2:
            block = c2.enter_context(nc.Block(name="sa_attend"))
            hs = lambda a: a.rearrange("p (h s) -> p h s", h=H)

            @block.tensor
            def _(pe):
                for b in range(4):
                    for k in range(2):
                        pe.transpose((B0, B1)[k][:, 128 * b:128 * b + 128], A[:, b, 128 * k:128 * k + 128], g.ident[:, :])
                    ins = pe.transpose(B2[0:1, 128 * b:128 * b + 128], A[:, b, D:D + 1], g.ident[:, :])
                ins.then_inc(s_pe, 1)
                pe.wait_ge(s_out, 1)
                for n in range(H):
                    c = slice(S * n, S * n + S)
                    ins = matmul_k(pe, B3[:S, c], [w.fx[:, 0, c], w.fx[:, 1, c], w.bfx[0:1, c]],
                                   [AT[:, 0, c], AT[:, 1, c], nT[:, c]])
                ins.then_inc(s_pe, 1)
                pe.wait_ge(s_out, 2)
                pe.matmul(B0[:S, :], w.q[:, :], TT[:, :], start=True, stop=True)
                pe.matmul(B1[:S, :], w.k[:, :], TT[:, :], start=True, stop=True)
                for n in range(H):
                    c = slice(S * n, S * n + S)
                    ins = pe.matmul(B2[:S, c], TT[:, c], w.v[:, :], start=True, stop=True)
                ins.then_inc(s_pe, 1)
                pe.wait_ge(s_out, 3)
                for n in range(H):
                    c = slice(S * n, S * n + S)
                    ins = pe.matmul(B3[:S, c], qT[:, c], kT[:, c], start=True, stop=True)
                ins.then_inc(s_pe, 1)
                pe.wait_ge(s_out, 4)
                for n in range(H):
                    c = slice(S * n, S * n + S)
                    ins = pe.transpose(B0[:S, c], at[:, c], g.ident[:S, :S])
                ins.then_inc(s_pe, 1)
                pe.wait_ge(s_out, 5)
                for n in range(H):
                    c = slice(S * n, S * n + S)
                    ins = pe.matmul(B1[:S, c], v_[:, c], atT[:, c], start=True, stop=True)
                ins.then_inc(s_pe, 1)
                pe.wait_ge(s_out, 6)
                for n in range(H):
                    bank = (B2, B3)[n // 4]
                    p, c = S * (n % 2), D * ((n // 2) % 2)
                    ins = pe.matmul(bank[p:p + S, c:c + D], oT[:, S * n:S * n + S], w.out[:, n, :],
                                    start=True, stop=True)
                ins.then_inc(s_pe, 1)

            @block.scalar
            def _(act):
                act.wait_ge(s_act, 1)
                act.activation(at[:, :], at[:, :], ACT.Exp).then_inc(s_act, 1)

            @block.vector
            def _(dve):
                st = Steps(dve, s_st, 5)
                dve.wait_ge(s_pe, 1)
                dve.tensor_copy(AT[:, 0, :], B0[:, :])
                dve.tensor_copy(AT[:, 1, :], B1[:, :])
                dve.tensor_copy(nT[:, :], B2[0:1, :]).then_inc(s_out, 1)
                dve.wait_ge(s_pe, 2)
                dve.tensor_copy(TT[:, :], B3[:S, :]).then_inc(s_out, 1)
                dve.wait_ge(s_pe, 3)
                dve.tensor_copy(qT[:, :], B0[:S, :])
                dve.tensor_copy(kT[:, :], B1[:S, :])
                dve.tensor_copy(v_[:, :], B2[:S, :]).then_inc(s_out, 1)
                dve.wait_ge(s_pe, 4)
                st.link(dve.tensor_reduce(top[:, :], hs(B3[:S, :]), AX, ALU.max))
                st.link(dve.tensor_tensor(hs(at[:, :]), hs(B3[:S, :]), top[:, :].unsqueeze(2).broadcast_to([S, H, S]),
                                          ALU.subtract))
                dve.tensor_scalar(at[:, :], at[:, :], S ** -0.5, None, ALU.mult).then_inc(s_act, 1)
                dve.wait_ge(s_act, 2)
                st.link(dve.tensor_reduce(top[:, :], hs(at[:, :]), AX, ALU.add))
                st.link(dve.reciprocal(top[:, :], top[:, :]))
                dve.tensor_tensor(hs(at[:, :]), hs(at[:, :]), top[:, :].unsqueeze(2).broadcast_to([S, H, S]),
                                  ALU.mult).then_inc(s_out, 1)
                dve.wait_ge(s_pe, 5)
                dve.tensor_copy(atT[:, :], B0[:S, :]).then_inc(s_out, 1)
                dve.wait_ge(s_pe, 6)
                dve.tensor_copy(oT[:, :], B1[:S, :]).then_inc(s_out, 1)
                dve.wait_ge(s_pe, 7)
                dve.tensor_copy(w.ow[:, 0:2, :], B2[:, :].rearrange("p (b n) -> p b n", b=2))
                dve.tensor_copy(w.ow[:, 2:4, :], B3[:, :].rearrange("p (b n) -> p b n", b=2))


def slice_output_phase(nc, g, w):
    with ExitStack() as ctx:
        m = Mem(nc, ctx)
        wt = m.sb("so_wt", [128, 2, 8 * S])
        wT = m.sb("so_wT", [128, 2, 4, P])
        y = m.sb("so_y", [128, 2, D])
        T = [m.bank(f"so_T{j}") for j in range(2)]
        Y = m.bank("so_Y")
        s_wt, s_y, s_st, s_read = (m.sem(f"so_{n}") for n in ("wt", "y", "st", "read"))
        s_tr = [m.sem(f"so_tr{j}") for j in range(2)]
        s_wT = [m.sem(f"so_wT{j}") for j in range(2)]
        block = ctx.enter_context(nc.Block())

        @block.scalar
        def _(act):
            with act.Fori(0, PAIRS) as i:
                v = i + 1
                act.activation(wt[:P, :, :], g.W[:P, ds(2 * i, 2), :], ACT.Identity).then_inc(s_wt, 1)
                for j in range(2):
                    act.wait_ge(s_tr[j], v)
                    act.activation(wT[:, j, :, :], T[j][:, 0:4 * P].rearrange("p (b n) -> p b n", b=4),
                                   ACT.Identity).then_inc(s_wT[j], 1)

        @block.vector
        def _(dve):
            with dve.Fori(0, PAIRS) as i:
                st = Steps(dve, s_st, i)
                dve.wait_ge(s_y, i + 1)
                dve.tensor_tensor(y[:P, :, :], Y[:P, :].rearrange("p (j n) -> p j n", j=2),
                                  w.bout[:P, :].unsqueeze(1).broadcast_to([P, 2, D]), ALU.add)\
                   .then_inc(s_read, 1)
                dve.wait_ge(s_read, i + 2)
                st.link(dve.tensor_tensor(g.X[:P, ds(2 * i, 2), :], y[:P, :, :], g.X[:P, ds(2 * i, 2), :], ALU.add))
                for j in range(2):
                    dve.bn_stats(g.halves[:P, ds(2 * i + j, 1), :], g.X[:P, ds(2 * i + j, 1), :])

        @block.tensor
        def _(pe):
            pe.sem_inc(s_read, 1)
            with pe.Fori(0, PAIRS) as i:
                v = i + 1
                pe.wait_ge(s_wt, v)
                for j in range(2):
                    for b in range(4):
                        ins = pe.transpose(T[j][:, b * P:(b + 1) * P], wt[:P, j, 128 * b:128 * b + 128],
                                           g.ident[:P, :P])
                    ins.then_inc(s_tr[j], 1)
                pe.wait_ge(s_read, v)
                for j in range(2):
                    pe.wait_ge(s_wT[j], v)
                    ins = matmul_k(pe, Y[:P, j * D:(j + 1) * D], [wT[:, j, b, :] for b in range(4)],
                                   [w.ow[:, b, :] for b in range(4)])
                ins.then_inc(s_y, 1)
def mixer1_sums_phase(nc, g, w, KV):
    with ExitStack() as ctx:
        m = Mem(nc, ctx)
        xn = m.sb("m1_xn", [128, 2, D])
        xnT = m.sb("m1_xnT", [128, 2, 2 * P])
        kv = m.sb("m1_kv", [128, 2, 2 * D])
        sq = m.sb("m1_sq", [128, 2, 2 * D])
        kvn = m.sb("m1_kvn", [128, 2, 2 * D])
        mean, var, root = (m.sb(f"m1_{n}", [128, 32]) for n in ("mean", "var", "root"))
        T = m.bank("m1_T")
        Q = [m.bank(f"m1_Q{j}") for j in range(2)]
        names = ("xn", "tr", "xnT", "kv", "cen", "sq", "var", "root", "n", "aff", "sum", "out", "st")
        s = {n: m.sem(f"m1_{n}") for n in names}
        block = ctx.enter_context(nc.Block())
        heads = lambda a: a.rearrange("p j (h c) -> p (j h) c", c=HD)
        per_head = lambda a: a[:P, :].unsqueeze(2).broadcast_to([P, 32, HD])
        both = lambda a: a[:P, :].unsqueeze(1).broadcast_to([P, 2, 2 * D])

        @block.sync
        def _(sp):
            with sp.Fori(0, PAIRS) as i:
                sp.wait_ge(s["xn"], i + 1)
                sp.dma_start(g.table1.rearrange("(t p) n -> p t n", p=P)[:, ds(2 * i, 2), :], xn[:P, :, :])\
                  .then_inc(s["out"], 16)
            sp.wait_ge(s["out"], 16 * PAIRS + 16)

        @block.scalar
        def _(act):
            act.sem_inc(s["out"], 16)
            with act.Fori(0, PAIRS) as i:
                v = i + 1
                act.wait_ge(s["out"], 16 * i + 16)
                normalise(act, g, g.X, xn, i, g.rstd, g.shift).then_inc(s["xn"], 1)
                act.wait_ge(s["cen"], v)
                act.activation(sq[:P, :, :], kv[:P, :, :], ACT.Square).then_inc(s["sq"], 1)
                act.wait_ge(s["var"], v)
                act.activation(root[:P, :], var[:P, :], ACT.Sqrt).then_inc(s["root"], 1)

        @block.vector
        def _(dve):
            with dve.Fori(0, PAIRS) as i:
                v = i + 1
                st = Steps(dve, s["st"], i * 7)
                dve.wait_ge(s["tr"], v)
                dve.tensor_copy(xnT[:, :, :], pair_blocks(T)).then_inc(s["xnT"], 1)
                dve.wait_ge(s["kv"], v)
                for j in range(2):
                    st.mark(dve.tensor_tensor(kv[:P, j, :], Q[j][:P, :], w.bkv[:P, :], ALU.add))
                st.wait()
                st.link(dve.tensor_reduce(mean[:P, :], heads(kv[:P, :, :]), AX, ALU.add))
                st.link(dve.tensor_scalar(mean[:P, :], mean[:P, :], 1.0 / HD, None, ALU.mult))
                dve.tensor_tensor(heads(kv[:P, :, :]), heads(kv[:P, :, :]), per_head(mean), ALU.subtract)\
                   .then_inc(s["cen"], 1)
                dve.wait_ge(s["sq"], v)
                st.link(dve.tensor_reduce(var[:P, :], heads(sq[:P, :, :]), AX, ALU.add))
                dve.tensor_scalar(var[:P, :], var[:P, :], 1.0 / HD, EPS, ALU.mult, ALU.add).then_inc(s["var"], 1)
                dve.wait_ge(s["root"], v)
                st.link(dve.reciprocal(root[:P, :], root[:P, :]))
                dve.wait_ge(s["sum"], v)
                dve.tensor_tensor(heads(kvn[:P, :, :]), heads(kv[:P, :, :]), per_head(root), ALU.mult)\
                   .then_inc(s["n"], 1)
                dve.wait_ge(s["n"], v)
                st.link(dve.tensor_tensor(kvn[:P, :, :], kvn[:P, :, :], both(w.kvg), ALU.mult))
                dve.tensor_tensor(kvn[:P, :, :], kvn[:P, :, :], both(w.kvb), ALU.add).then_inc(s["aff"], 1)

        @block.tensor
        def _(pe):
            pe.matmul(KV[:, :], g.zeros[:, 0:128], g.zeros[:, :], start=True, stop=False)
            pe.sem_inc(s["sum"], 1)
            with pe.Fori(0, PAIRS) as i:
                v = i + 1
                pe.wait_ge(s["xn"], v)
                turn_pair(pe, g, T, xn).then_inc(s["tr"], 1)
                pe.wait_ge(s["xnT"], v)
                for j in range(2):
                    ins = matmul_k(pe, Q[j][:P, :], tile_of(xnT, j), [w.kv[:, b, :] for b in range(2)])
                ins.then_inc(s["kv"], 1)
                pe.wait_ge(s["aff"], v)
                for j in range(2):
                    for b in range(2):
                        c = slice(128 * b, 128 * b + 128)
                        ins = pe.matmul(KV[:, c], kvn[:P, j, c], kvn[:P, j, D + 128 * b:D + 128 * b + 128],
                                        start=False, stop=False, skip_group_check=True)
                ins.then_inc(s["sum"], 1)
            pe.matmul(KV[:, :], g.zeros[:, 0:128], g.zeros[:, :], start=False, stop=True)


def fold1_phase(nc, g, w, KV):
    with ExitStack() as ctx:
        m = Mem(nc, ctx)
        kvd = m.sb("f1_kvd", [128, 2, 128])
        PW, PB, PR0, PR1 = (m.bank(f"f1_{n}") for n in ("W", "B", "R0", "R1"))
        s_zero, s_kvd, s_mm = (m.sem(f"f1_{n}") for n in ("zero", "kvd", "mm"))
        block = ctx.enter_context(nc.Block())

        @block.gpsimd
        def _(pool):
            pool.memset(kvd[:, :, :], 0.0).then_inc(s_zero, 1)

        @block.vector
        def _(dve):
            dve.tensor_tensor(w.brz[:, :], w.brz[:, :], w.bhrz[:, :], ALU.add)
            dve.wait_ge(s_zero, 1)
            for b in range(2):
                for h in range(4):
                    p = slice(HD * h, HD * h + HD)
                    ins = dve.tensor_scalar(kvd[p, b, p], KV[p, 128 * b + HD * h:128 * b + HD * h + HD],
                                            1.0 / N, None, ALU.mult)
            ins.then_inc(s_kvd, 1)
            dve.wait_ge(s_mm, 1)
            dve.tensor_copy(w.qkv[:, :, :], PW[:, :].rearrange("p (b n) -> p b n", b=2))
            dve.tensor_copy(w.bqkv[:, :], PB[:, 0:2])
            dve.tensor_copy(w.relw[:, 0:512], PR0[:NREL, :])
            dve.tensor_copy(w.relw[:, 512:768], PR1[:NREL, 0:256])

        @block.tensor
        def _(pe):
            matmul_k(pe, PR0[:NREL, :], [w.relT[:, b, :] for b in range(2)], [w.ih[:, b, 0:512] for b in range(2)])
            matmul_k(pe, PR1[:NREL, 0:256], [w.relT[:, b, :] for b in range(2)],
                     [w.ih[:, b, 512:768] for b in range(2)])
            pe.wait_ge(s_kvd, 1)
            for b in range(2):
                for k in range(2):
                    pe.matmul(PW[:, k * D + 128 * b:k * D + 128 * b + 128], w.qT[:, b, 128 * k:128 * k + 128],
                              kvd[:, b, :], start=True, stop=True)
                ins = pe.matmul(PB[:, b:b + 1], kvd[:, b, :], w.bq[:, b:b + 1], start=True, stop=True)
            ins.then_inc(s_mm, 1)


def layer1_dense_phase(nc, g, w):
    with ExitStack() as ctx:
        m = Mem(nc, ctx)
        xn = m.sb("l1_xn", [128, 2, D])
        red = m.sb("l1_red", [128, 2, RELW])
        xnT, redT, retT, hT = (m.sb(f"l1_{n}", [128, 2, 2 * P]) for n in ("xnT", "redT", "retT", "hT"))
        cntT = m.sb("l1_cntT", [NREL, 2 * P])
        rz = m.sb("l1_rz", [128, 2, 512])
        nn = m.sb("l1_nn", [128, 2, D])
        u = m.sb("l1_u", [128, 2, D])
        RZ = [m.bank(f"l1_RZ{j}") for j in range(2)]
        NN = [m.bank(f"l1_NN{j}") for j in range(2)]
        TX, TR, TC, M = (m.bank(f"l1_{n}") for n in ("TX", "TR", "TC", "M"))
        names = ("xn", "red", "tx", "tr", "xnT", "redT", "gates", "ret", "retT", "h", "hT", "y", "rz", "sig", "pre",
                 "tanh", "st", "u", "x")
        s = {n: m.sem(f"l1_{n}") for n in names}
        block = ctx.enter_context(nc.Block())
        both = lambda a: a[:P, :].unsqueeze(1).broadcast_to([P, 2, D])

        @block.scalar
        def _(act):
            with act.Fori(0, PAIRS) as i:
                v = i + 1
                normalise(act, g, g.X, xn, i, g.rstd, g.shift).then_inc(s["xn"], 1)
                act.activation(red[:P, :, :], g.red[:P, ds(2 * i, 2), :], ACT.Identity).then_inc(s["red"], 1)
                act.wait_ge(s["tx"], v)
                act.activation(xnT[:, :, :], pair_blocks(TX), ACT.Identity).then_inc(s["xnT"], 1)
                act.wait_ge(s["rz"], v)
                act.activation(rz[:P, :, :], rz[:P, :, :], ACT.Sigmoid).then_inc(s["sig"], 1)
                act.wait_ge(s["pre"], v)
                act.activation(nn[:P, :, :], nn[:P, :, :], ACT.Tanh).then_inc(s["tanh"], 1)
                act.wait_ge(s["h"], v)
                for b in range(2):
                    ins = act.activation(hT[:, b, :], pair_blocks(TX)[:, b, :], ACT.Gelu, bias=w.b1[:, b:b + 1])
                ins.then_inc(s["hT"], 1)
                act.wait_ge(s["st"], 8 * v)

        @block.vector
        def _(dve):
            with dve.Fori(0, PAIRS) as i:
                v = i + 1
                st = Steps(dve, s["st"], i * 8)
                dve.wait_ge(s["tr"], v)
                dve.tensor_copy(cntT[:, :], TC[:NREL, 0:2 * P])
                dve.tensor_copy(redT[:, :, :], pair_blocks(TR)).then_inc(s["redT"], 1)
                dve.wait_ge(s["ret"], v)
                for b in range(2):
                    ins = dve.scalar_tensor_tensor(retT[:, b, :], pair_blocks(M)[:, b, :], w.bqkv[:, b:b + 1],
                                                   xnT[:, b, :], ALU.add, ALU.add)
                ins.then_inc(s["retT"], 1)
                dve.wait_ge(s["gates"], v)
                for j in range(2):
                    ins = dve.tensor_tensor(rz[:P, j, :], RZ[j][:P, :], w.brz[:P, :], ALU.add)
                ins.then_inc(s["rz"], 1)
                for j in range(2):
                    st.mark(dve.tensor_tensor(nn[:P, j, :], NN[j][:P, D:2 * D], w.bhn[:P, :], ALU.add))
                    st.mark(dve.tensor_tensor(u[:P, j, :], NN[j][:P, 0:D], w.bin[:P, :], ALU.add))
                dve.wait_ge(s["sig"], v)
                st.wait()
                st.link(dve.tensor_tensor(nn[:P, :, :], nn[:P, :, :], rz[:P, :, 0:D], ALU.mult))
                dve.tensor_tensor(nn[:P, :, :], nn[:P, :, :], u[:P, :, :], ALU.add).then_inc(s["pre"], 1)
                dve.wait_ge(s["tanh"], v)
                st.link(dve.tensor_tensor(u[:P, :, :], xn[:P, :, :], nn[:P, :, :], ALU.subtract))
                st.link(dve.tensor_tensor(u[:P, :, :], u[:P, :, :], rz[:P, :, D:2 * D], ALU.mult))
                dve.tensor_tensor(u[:P, :, :], u[:P, :, :], nn[:P, :, :], ALU.add).then_inc(s["u"], 1)
                dve.wait_ge(s["u"], 3 * i + 1)
                dve.tensor_tensor(u[:P, :, :], u[:P, :, :], xn[:P, :, :], ALU.add).then_inc(s["u"], 1)
                dve.wait_ge(s["u"], 3 * i + 2)
                dve.tensor_tensor(u[:P, :, :], u[:P, :, :], both(w.b2), ALU.add).then_inc(s["u"], 1)
                dve.wait_ge(s["y"], v)
                dve.wait_ge(s["u"], 3 * i + 3)
                st.link(dve.tensor_tensor(u[:P, :, :], M[:P, :].rearrange("p (j n) -> p j n", j=2), u[:P, :, :],
                                          ALU.add))
                dve.tensor_tensor(g.X[:P, ds(2 * i, 2), :], u[:P, :, :], g.X[:P, ds(2 * i, 2), :], ALU.add)\
                   .then_inc(s["x"], 1)
                dve.wait_ge(s["x"], v)
                for j in range(2):
                    dve.bn_stats(g.halves[:P, ds(2 * i + j, 1), :], g.X[:P, ds(2 * i + j, 1), :])

        @block.tensor
        def _(pe):
            with pe.Fori(0, PAIRS) as i:
                v = i + 1
                pe.wait_ge(s["xn"], v)
                turn_pair(pe, g, TX, xn).then_inc(s["tx"], 1)
                pe.wait_ge(s["red"], v)
                for j in range(2):
                    for b in range(2):
                        pe.transpose(TR[:, (2 * b + j) * P:(2 * b + j + 1) * P], red[:P, j, 128 * b:128 * b + 128],
                                     g.ident[:P, :P])
                    ins = pe.transpose(TC[:NREL, j * P:(j + 1) * P], red[:P, j, D:RELW], g.ident[:P, :P])
                ins.then_inc(s["tr"], 1)
                pe.wait_ge(s["xnT"], v)
                for c in range(2):
                    ins = matmul_k(pe, M[:, c * 2 * P:(c + 1) * 2 * P],
                                   [w.qkv[:, b, 128 * c:128 * c + 128] for b in range(2)],
                                   [xnT[:, b, :] for b in range(2)])
                ins.then_inc(s["ret"], 1)
                pe.wait_ge(s["redT"], v)
                for j in range(2):
                    x, r, c = tile_of(xnT, j), tile_of(redT, j), cntT[:, j * P:(j + 1) * P]
                    matmul_k(pe, RZ[j][:P, :], x + r + [c],
                             [w.hh[:, b, 0:512] for b in range(2)] + [w.ih[:, b, 0:512] for b in range(2)]
                             + [w.relw[:, 0:512]])
                    matmul_k(pe, NN[j][:P, 0:D], r + [c],
                             [w.ih[:, b, 512:768] for b in range(2)] + [w.relw[:, 512:768]])
                    ins = matmul_k(pe, NN[j][:P, D:2 * D], x, [w.hh[:, b, 512:768] for b in range(2)])
                ins.then_inc(s["gates"], 1)
                pe.wait_ge(s["retT"], v)
                for c in range(2):
                    ins = matmul_k(pe, TX[:, c * 2 * P:(c + 1) * 2 * P],
                                   [w.w1[:, b, 128 * c:128 * c + 128] for b in range(2)],
                                   [retT[:, b, :] for b in range(2)])
                ins.then_inc(s["h"], 1)
                pe.wait_ge(s["hT"], v)
                for j in range(2):
                    ins = matmul_k(pe, M[:P, j * D:(j + 1) * D], tile_of(hT, j), [w.w2[:, b, :] for b in range(2)])
                ins.then_inc(s["y"], 1)


def experts_phase(nc, g, w, out):
    with ExitStack() as ctx:
        m = Mem(nc, ctx)
        xn = m.sb("ex_xn", [128, 2, D])
        xnT = m.sb("ex_xnT", [128, 2, 2 * P])
        h = [m.sb(f"ex_h{a}", [128, 2, 2 * P]) for a in range(2)]
        lg, e8, top, cmb, hit = (m.sb(f"ex_{n}", [128, 2, NEXP]) for n in ("lg", "e8", "top", "cmb", "hit"))
        pos = m.sb("ex_pos", [128, 2, NEXP], U32)
        posf = m.sb("ex_posf", [128, 2, NEXP])
        tot = m.sb("ex_tot", [128, 2])
        cmbT = m.sb("ex_cmbT", [NEXP, 2 * P])
        acc = m.sb("ex_acc", [128, 2, D])
        T, B, R = m.bank("ex_T"), m.bank("ex_B"), m.bank("ex_R")
        HB = [m.bank(f"ex_H{a}") for a in range(2)]
        YB = [m.bank(f"ex_Y{a}") for a in range(2)]
        names = ("xn", "tr", "xnT", "lg", "max", "exp", "cmb", "ct", "cmbT", "b", "hb", "h", "y", "used", "acc", "out",
                 "st", "seen")
        s = {n: m.sem(f"ex_{n}") for n in names}
        block = ctx.enter_context(nc.Block())

        @block.sync
        def _(sp):
            with sp.Fori(0, PAIRS) as i:
                sp.wait_ge(s["acc"], i + 1)
                sp.dma_start(out.rearrange("(t p) n -> p t n", p=P)[:, ds(2 * i, 2), :], acc[:P, :, :])\
                  .then_inc(s["out"], 16)
            sp.wait_ge(s["out"], 16 * PAIRS + 16)

        @block.scalar
        def _(act):
            act.sem_inc(s["out"], 16)
            with act.Fori(0, PAIRS) as i:
                v = i + 1
                normalise(act, g, g.X, xn, i, g.rstd, g.shift).then_inc(s["xn"], 1)
                act.wait_ge(s["max"], v)
                act.activation(e8[:P, :, :], lg[:P, :, :], ACT.Exp).then_inc(s["exp"], 1)
                for e in range(NEXP):
                    act.wait_ge(s["hb"], NEXP * i + e + 1)
                    for b in range(2):
                        ins = act.activation(h[e % 2][:, b, :], pair_blocks(HB[e % 2])[:, b, :], ACT.Gelu,
                                             bias=w.b1[:, 2 * e + b:2 * e + b + 1])
                    ins.then_inc(s["h"], 1)
                act.wait_ge(s["acc"], v)

        @block.vector
        def _(dve):
            with dve.Fori(0, PAIRS) as i:
                v = i + 1
                st = Steps(dve, s["st"], i * 15)
                dve.wait_ge(s["tr"], v)
                dve.tensor_copy(xnT[:, :, :], pair_blocks(T)).then_inc(s["xnT"], 1)
                dve.wait_ge(s["lg"], v)
                st.link(dve.tensor_copy(e8[:P, :, :], R[:P, 0:2 * NEXP].rearrange("p (j n) -> p j n", j=2)))
                dve.sem_inc(s["seen"], 1)
                for j in range(2):
                    st.mark(dve.max(top[:P, j, :], e8[:P, j, :]))
                st.wait()
                dve.sem_inc(s["seen"], 1)
                for j in range(2):
                    st.mark(dve.max_index(pos[:P, j, :], top[:P, j, :], e8[:P, j, :]))
                st.wait()
                st.mark(dve.tensor_copy(posf[:P, :, :], pos[:P, :, :]))
                dve.tensor_tensor(lg[:P, :, :], top[:P, :, :], top[:P, :, 0:1].broadcast_to([P, 2, NEXP]),
                                  ALU.subtract).then_inc(s["max"], 1)
                dve.wait_ge(s["exp"], v)
                st.link(dve.tensor_tensor(tot[:P, :].unsqueeze(2), e8[:P, :, 0:1], e8[:P, :, 1:2], ALU.add))
                st.link(dve.reciprocal(tot[:P, :], tot[:P, :]))
                st.link(dve.tensor_tensor(e8[:P, :, 0:2], e8[:P, :, 0:2],
                                          tot[:P, :].unsqueeze(2).broadcast_to([P, 2, 2]), ALU.mult))
                for j in range(2):
                    for k, to in enumerate((cmb, hit)):
                        st.mark(dve.tensor_scalar(to[:P, j, :], g.iota[:P, 0:NEXP], posf[:P, j, k:k + 1],
                                                  e8[:P, j, k:k + 1], ALU.is_equal, ALU.mult))
                st.wait()
                dve.tensor_tensor(cmb[:P, :, :], cmb[:P, :, :], hit[:P, :, :], ALU.add).then_inc(s["cmb"], 1)
                dve.wait_ge(s["ct"], v)
                dve.tensor_copy(cmbT[:, :], R[:NEXP, 256:256 + 2 * P]).then_inc(s["cmbT"], 1)
                dve.wait_ge(s["b"], v)
                dve.wait_ge(s["out"], 16 * i + 16)
                st.link(dve.tensor_tensor(acc[:P, :, :], B[:P, :].rearrange("p (j n) -> p j n", j=2), xn[:P, :, :],
                                          ALU.add))
                st.link(dve.tensor_tensor(acc[:P, :, :], acc[:P, :, :], g.X[:P, ds(2 * i, 2), :], ALU.add))
                for e in range(NEXP):
                    dve.wait_ge(s["y"], NEXP * i + e + 1)
                    for j in range(2):
                        ins = dve.scalar_tensor_tensor(acc[:P, j, :], YB[e % 2][:P, j * D:(j + 1) * D],
                                                       cmb[:P, j, e:e + 1], acc[:P, j, :], ALU.mult, ALU.add)
                    ins.then_inc(s["used"], 1)
                    dve.wait_ge(s["used"], NEXP * i + e + 1)
                dve.sem_inc(s["acc"], 1)

        @block.tensor
        def _(pe):
            def expert_out(i, e):
                pe.wait_ge(s["h"], NEXP * i + e + 1)
                ins = None
                for j in range(2):
                    ins = matmul_k(pe, YB[e % 2][:P, j * D:(j + 1) * D], tile_of(h[e % 2], j),
                                   [w.w2[:, 2 * e + b, :] for b in range(2)])
                ins.then_inc(s["y"], 1)

            with pe.Fori(0, PAIRS) as i:
                v = i + 1
                pe.wait_ge(s["xn"], v)
                turn_pair(pe, g, T, xn).then_inc(s["tr"], 1)
                pe.wait_ge(s["xnT"], v)
                for j in range(2):
                    ins = matmul_k(pe, R[:P, j * NEXP:(j + 1) * NEXP], tile_of(xnT, j), [w.rt[:, b, :] for b in range(2)])
                ins.then_inc(s["lg"], 1)
                for e in range(NEXP):
                    for c in range(2):
                        ins = matmul_k(pe, HB[e % 2][:, c * 2 * P:(c + 1) * 2 * P],
                                       [w.w1[:, 2 * e + b, 128 * c:128 * c + 128] for b in range(2)],
                                       [xnT[:, b, :] for b in range(2)])
                    ins.then_inc(s["hb"], 1)
                    if e == 1:
                        pe.wait_ge(s["cmb"], v)
                        for j in range(2):
                            ins = pe.transpose(R[:NEXP, 256 + j * P:256 + (j + 1) * P], cmb[:P, j, :], g.ident[:P, :P])
                        ins.then_inc(s["ct"], 1)
                    if e == 2:
                        pe.wait_ge(s["cmbT"], v)
                        for j in range(2):
                            ins = pe.matmul(B[:P, j * D:(j + 1) * D], cmbT[:, j * P:(j + 1) * P], w.b2[:, :],
                                            start=True, stop=True)
                        ins.then_inc(s["b"], 1)
                    if e >= 1:
                        if e >= 3:
                            pe.wait_ge(s["used"], NEXP * i + e - 2)
                        expert_out(i, e - 1)
                pe.wait_ge(s["used"], NEXP * i + NEXP - 2)
                expert_out(i, NEXP - 1)
                pe.wait_ge(s["acc"], v)
class Names:
    pass


def build(nc, a, table0, table1, out):
    tiles = lambda x: x.rearrange("(t p) c -> p t c", p=P)
    with ExitStack() as ctx:
        m = Mem(nc, ctx)
        g = Names()
        g.table0, g.table1, g.dst_groups = table0, table1, a["dst_groups"]
        g.X = m.sb("X", [128, NT, D])
        g.halves = m.sb("halves", [128, NT, 6])
        g.rstd, g.shift = m.sb("rstd", [128, NT]), m.sb("shift", [128, NT])
        g.ident, g.ones, g.zeros = m.sb("ident", [128, 128]), m.sb("ones", [128, 1]), m.sb("zeros", [128, 512])
        g.iota_i, g.iota = m.sb("iota_i", [128, 256], I32), m.sb("iota", [128, 256])
        g.chan_i, g.chan = m.sb("chan_i", [128, 1], I32), m.sb("chan", [128, 1])
        g.tile_i, g.tile0 = m.sb("tile_i", [128, NT], I32), m.sb("tile0", [128, NT])
        g.before = m.sb("before", [128, NT])
        g.src_i = m.sb("src_i", [128, NG * ET], I32)
        g.dst, g.rel = m.sb("dst", [128, NG * ET]), m.sb("rel", [128, NG * ET])
        g.visits = m.sb("visits", [1, NT, 3], I32)

        constants_phase(nc, g)
        with ExitStack() as c:
            m0 = Mem(nc, c)
            g.dst_i, g.rel_i = m0.sb("dst_i", [128, NG * ET], I32), m0.sb("rel_i", [128, NG * ET], I32)
            load_phase(nc, "ld_edges", [(g.src_i[:P, :], a["src_e"]), (g.dst_i[:P, :], a["dst_e"]),
                                        (g.rel_i[:P, :], a["rel_e"])])
            edge_lists_phase(nc, g)
        ranges_phase(nc, g)

        with ExitStack() as c:
            m1 = Mem(nc, c)
            w = Names()
            g.asad = m1.sb("asad", [128, NT, 16])
            g.tdst, g.wself = m1.sb("tdst", [128, NT, 16]), m1.sb("wself", [128, NT, H])
            g.R, g.rhalves = m1.sb("R", [128, NT, D]), m1.sb("rhalves", [128, NT, 6])
            g.rrstd, g.rshift = m1.sb("rrstd", [128, NT]), m1.sb("rshift", [128, NT])
            w.cat, w.kq = m1.sb("w_cat", [128, 2, D + 16]), m1.sb("w_kq", [128, 6, D])
            w.att, w.bv = m1.sb("w_att", [128, 2, 16]), m1.sb("w_bv", [128, 2])
            w.WT, w.vT, w.o, w.vo, w.mwo, w.w1, w.w2 = (
                m1.sb(f"w_{n}", [128, 2, D]) for n in ("WT", "vT", "o", "vo", "mwo", "w1", "w2"))
            w.bvo, w.b2, w.bo, w.bsum, w.gbias = (
                m1.sb(f"w_{n}", [128, D]) for n in ("bvo", "b2", "bo", "bsum", "gbias"))
            w.b1, w.lng, w.lnb = (m1.sb(f"w_{n}", [128, 2]) for n in ("b1", "lng", "lnb"))
            wq, bq = a["L0_mix_W_qkv"], a["L0_mix_b_qkv"]
            load_phase(nc, "ld_0", [(g.X[:P, 10 * n:10 * n + 10, :], tiles(a["x"])[:, 10 * n:10 * n + 10, :])
                                    for n in range(NT // 10)] + [
                (w.cat[:, :, 0:D], rows(a["L0_gnn_W"])), (w.att[:, :, :], rows(a["att"])),
                (w.WT[:, :, :], rows(a["WT"])), (w.kq[:, 0:2, :], rows(wq[:, D:2 * D])),
                (w.kq[:, 3:5, :], rows(wq[:, 0:D])), (w.kq[:, 2, :], wide(bq[D:2 * D])),
                (w.kq[:, 5, :], wide(bq[0:D])), (w.vT[:, :, :], rows(a["vT"])),
                (w.o[:, :, :], rows(a["L0_mix_W_out"])), (w.bv[:, :], a["bv_cols"]),
                (w.b2[:, :], wide(a["L0_gnn_b2"])), (w.bo[:, :], wide(a["L0_mix_b_out"])),
                (w.w1[:, :, :], rows(a["L0_gnn_W1"])), (w.w2[:, :, :], rows(a["L0_gnn_W2"])),
                (w.gbias[:, :], wide(a["L0_gnn_bias"])), (w.b1[:, :], a["gb1_cols"]),
                (w.lng[:, :], a["lng_cols"]), (w.lnb[:, :], a["lnb_cols"])])
            first_stats_phase(nc, g)
            scales_phase(nc, "sc0", g.halves, g.rstd, g.shift)
            fold0_phase(nc, g, w)
            with ExitStack() as c2:
                G0, G1 = Mem(nc, c2).bank("G0"), Mem(nc, c2).bank("G1")
                pass1_phase(nc, g, w, G0, G1)
                mixer0_fold_phase(nc, g, w, G0, G1)
            guard_phase(nc, g)
            attend_edges_phase(nc, g, w)
            scales_phase(nc, "scr", g.rhalves, g.rrstd, g.rshift)
            layer0_dense_phase(nc, g, w)
        scales_phase(nc, "sc1", g.halves, g.rstd, g.shift)

        with ExitStack() as c:
            m2 = Mem(nc, c)
            w = Names()
            g.W = m2.sb("W", [128, NT, 8 * S])
            w.ow, w.bout = m2.sb("w_ow", [128, 4, D]), m2.sb("w_bout", [128, D])
            with ExitStack() as c2:
                SL = [Mem(nc, c2).bank(f"SL{b}") for b in range(4)]
                with ExitStack() as c3:
                    m3 = Mem(nc, c3)
                    w.lg, w.lb = m3.sb("w_lg", [128, 2, 512]), m3.sb("w_lb", [128, 512])
                    w.bs, w.ws2 = m3.sb("w_bs", [128, S]), m3.sb("w_ws2", [128, 128])
                    w.bx, w.temp = m3.sb("w_bx", [128, 4]), m3.sb("w_temp", [128, H])
                    with ExitStack() as c4:
                        w.xT = Mem(nc, c4).sb("w_xT", [128, 4, D])
                        load_phase(nc, "ld_fs", [
                            (w.xT[:, :, :], rows(a["xT"])), (w.ws2[:, :], a["ws2"]), (w.bx[:, :], a["bx_cols"]),
                            (w.temp[:, :], wide(a["temp"])), (w.bs[:, :], wide(a["L0_ffn_b_slice"]))])
                        fold_slices_phase(nc, g, w)
                    slice_sums_phase(nc, g, w, SL)
                with ExitStack() as c3:
                    m3 = Mem(nc, c3)
                    w.fx, w.bfx, w.out = (m3.sb("w_fx", [128, 2, 512]), m3.sb("w_bfx", [1, 512]),
                                          m3.sb("w_out", [S, H, D]))
                    w.q, w.k, w.v = (m3.sb(f"w_s{n}", [S, S]) for n in ("q", "k", "v"))
                    load_phase(nc, "ld_sa", [
                        (w.fx[:, :, :], rows(a["L0_ffn_W_fx"])), (w.bfx[:, :], wide(a["L0_ffn_b_fx"], 1)),
                        (w.out[:, :, :], a["L0_ffn_W_out"].rearrange("(h s) n -> s h n", s=S)),
                        (w.q[:, :], a["L0_ffn_W_q"]), (w.k[:, :], a["L0_ffn_W_k"]), (w.v[:, :], a["L0_ffn_W_v"]),
                        (w.bout[:, :], wide(a["L0_ffn_b_out"]))])
                    slice_attention_phase(nc, g, w, SL)
            slice_output_phase(nc, g, w)
        scales_phase(nc, "sc2", g.halves, g.rstd, g.shift)

        with ExitStack() as c:
            m4 = Mem(nc, c)
            w = Names()
            g.red = m4.sb("red", [128, NT, RELW])
            w.kv, w.bkv = m4.sb("w_kv", [128, 2, 512]), m4.sb("w_bkv", [128, 512])
            w.kvg, w.kvb = m4.sb("w_kvg", [128, 512]), m4.sb("w_kvb", [128, 512])
            w.ih, w.hh = m4.sb("w_ih", [128, 2, 768]), m4.sb("w_hh", [128, 2, 768])
            w.relT, w.relw = m4.sb("w_relT", [128, 2, NREL]), m4.sb("w_relw", [NREL, 768])
            w.qT, w.qkv, w.w1, w.w2 = (m4.sb(f"w1_{n}", [128, 2, D]) for n in ("qT", "qkv", "w1", "w2"))
            w.bq, w.bqkv, w.b1 = (m4.sb(f"w1_{n}", [128, 2]) for n in ("bq", "bqkv", "b1"))
            w.brz, w.bhrz = m4.sb("w_brz", [128, 512]), m4.sb("w_bhrz", [128, 512])
            w.bin, w.bhn, w.b2 = (m4.sb(f"w1_{n}", [128, D]) for n in ("bin", "bhn", "b2"))
            bi, bh = a["L1_gnn_b_ih"], a["L1_gnn_b_hh"]
            load_phase(nc, "ld_1", [
                (w.kv[:, :, :], rows(a["m1_kv"])), (w.bkv[:, :], wide(a["m1_bkv"])),
                (w.ih[:, :, :], rows(a["w_ihT"])), (w.hh[:, :, :], rows(a["w_hhT"])),
                (w.relT[:, :, :], rows(a["relT"])), (w.qT[:, :, :], rows(a["m1_qT"])),
                (w.w1[:, :, :], rows(a["L1_mix_w1"])), (w.w2[:, :, :], rows(a["L1_mix_w2"])),
                (w.bq[:, :], a["m1_bq_cols"]), (w.b1[:, :], a["m1_b1_cols"]),
                (w.brz[:, :], wide(bi[0:512])), (w.bhrz[:, :], wide(bh[0:512])),
                (w.bin[:, :], wide(bi[512:768])), (w.bhn[:, :], wide(bh[512:768])),
                (w.b2[:, :], wide(a["L1_mix_b2"])),
                (w.kvg[:, :], wide(a["m1_kvg"])), (w.kvb[:, :], wide(a["m1_kvb"]))])
            with ExitStack() as c2:
                KV = Mem(nc, c2).bank("KV")
                mixer1_sums_phase(nc, g, w, KV)
                fold1_phase(nc, g, w, KV)
            relation_edges_phase(nc, g)
            layer1_dense_phase(nc, g, w)
        scales_phase(nc, "sc3", g.halves, g.rstd, g.shift)

        with ExitStack() as c:
            m5 = Mem(nc, c)
            w = Names()
            w.w1, w.w2 = m5.sb("we_1", [128, 2 * NEXP, D]), m5.sb("we_2", [128, 2 * NEXP, D])
            w.rt, w.b1, w.b2 = (m5.sb("we_rt", [128, 2, NEXP]), m5.sb("we_b1", [128, 2 * NEXP]),
                                m5.sb("we_b2", [NEXP, D]))
            load_phase(nc, "ld_ex", [
                (w.w1[:, :, :], rows(a["ex_w1"])), (w.w2[:, :, :], rows(a["ex_w2"])),
                (w.rt[:, :, :], rows(a["routerT"])), (w.b1[:, :], a["ex_b1_cols"]), (w.b2[:, :], a["L1_ffn_b2"])])
            experts_phase(nc, g, w, out)


def layouts(x):
    n = {k: np.ascontiguousarray(v) for k, v in x.items()}
    columns = lambda v: np.ascontiguousarray(v.reshape(-1, 128).T)
    edges = lambda v: np.ascontiguousarray(v.reshape(NG, P, ET).transpose(1, 0, 2).reshape(P, NG * ET))
    att = np.zeros((D, 2 * H), np.float32)
    for h in range(H):
        att[HD * h:HD * h + HD, h] = n["L0_gnn_att_src"][h]
        att[HD * h:HD * h + HD, H + h] = n["L0_gnn_att_dst"][h]
    ws2 = np.zeros((2 * S, 2 * S), np.float32)
    ws2[:S, :S] = ws2[S:, S:] = n["L0_ffn_W_slice"]
    qkv = n["L1_mix_w_qkv"].reshape(D, H, 3, HD)
    bqkv = n["L1_mix_b_qkv"].reshape(H, 3, HD)
    by_heads = lambda k, v: np.concatenate([np.tile(k, H), np.tile(v, H)])
    a = {k: n[k] for k in (
        "x", "L0_gnn_W", "L0_mix_W_qkv", "L0_mix_b_qkv", "L0_mix_W_out", "L0_mix_b_out", "L0_gnn_b2", "L0_gnn_W1",
        "L0_gnn_W2", "L0_gnn_bias", "L0_ffn_b_slice", "L0_ffn_W_fx", "L0_ffn_b_fx", "L0_ffn_W_out", "L0_ffn_W_q",
        "L0_ffn_W_k", "L0_ffn_W_v", "L0_ffn_b_out", "L1_gnn_b_ih", "L1_gnn_b_hh", "L1_mix_w1", "L1_mix_w2",
        "L1_mix_b2", "L1_ffn_b2")}
    a |= {
        "att": att, "WT": n["L0_gnn_W"].T, "vT": n["L0_mix_W_qkv"][:, 2 * D:].T,
        "bv_cols": columns(n["L0_mix_b_qkv"][2 * D:]), "gb1_cols": columns(n["L0_gnn_b1"]),
        "lng_cols": columns(n["L0_gnn_ln_g"]), "lnb_cols": columns(n["L0_gnn_ln_b"]),
        "src_e": edges(n["src"]), "dst_e": edges(n["dst"]), "rel_e": edges(n["edge_type_16"]),
        "dst_groups": n["dst"].reshape(2, NG // 2, EG).transpose(1, 0, 2),
        "xT": n["L0_ffn_W_x"].T, "ws2": ws2, "bx_cols": columns(n["L0_ffn_b_x"]),
        "temp": n["L0_ffn_temperature"].reshape(H),
        "m1_kv": np.concatenate([qkv[:, :, 1].reshape(D, D), qkv[:, :, 2].reshape(D, D)], 1),
        "m1_bkv": np.concatenate([bqkv[:, 1].reshape(D), bqkv[:, 2].reshape(D)]),
        "m1_qT": qkv[:, :, 0].reshape(D, D).T, "m1_bq_cols": columns(bqkv[:, 0].reshape(D)),
        "m1_b1_cols": columns(n["L1_mix_b1"]),
        "m1_kvg": by_heads(n["L1_mix_kln_g"], n["L1_mix_vln_g"]),
        "m1_kvb": by_heads(n["L1_mix_kln_b"], n["L1_mix_vln_b"]),
        "w_ihT": n["L1_gnn_w_ih"].T, "w_hhT": n["L1_gnn_w_hh"].T, "relT": n["L1_gnn_relvectors"].T,
        "ex_w1": n["L1_ffn_w1"].reshape(NEXP * D, D), "ex_w2": n["L1_ffn_w2"].reshape(NEXP * D, D),
        "routerT": n["L1_ffn_router_w"].T, "ex_b1_cols": columns(n["L1_ffn_b1"].reshape(-1)),
    }
    return {k: np.ascontiguousarray(v) for k, v in a.items()}


def kernel(**inputs):
    from concourse import bacc
    from concourse.bass_utils import run_bass_kernel_spmd

    nc = bacc.Bacc("TRN2", target_bir_lowering=False, num_devices=1)
    arrays = layouts({k: np.asarray(v) for k, v in inputs.items()})
    aps = {k: nc.dram_tensor(f"in_{k}", v.shape, mybir.dt.from_np(v.dtype), kind="ExternalInput").ap()
           for k, v in arrays.items()}
    out = nc.dram_tensor("out", (N, D), F32, kind="ExternalOutput").ap()
    table0 = nc.dram_tensor("table0", (N, GATW), F32).ap()
    table1 = nc.dram_tensor("table1", (N, D), F32).ap()
    build(nc, aps, table0, table1, out)
    r = run_bass_kernel_spmd(nc, [{f"in_{k}": v for k, v in arrays.items()}], core_ids=[0])
    return r.results[0]["out"]
```
